# Optimizing a Trainium2 kernel written in Bass

```python
import numpy as np
import jax
import jax.numpy as jnp

def _softmax(x, axis=-1):
    return jax.nn.softmax(x, axis=axis)

def _gelu(x):
    return jax.nn.gelu(x, approximate=True)

def _silu(x):
    return jax.nn.silu(x)

def _sigmoid(x):
    return jax.nn.sigmoid(x)

def _layernorm(x, axis=-1, eps=1e-05):
    m = jnp.mean(x, axis=axis, keepdims=True)
    v = jnp.var(x, axis=axis, keepdims=True)
    return (x - m) / jnp.sqrt(v + eps)

def _scatter_add(tgt, idx, src, axis=0):
    return tgt.at[idx].add(src)

def _segment_sum(src, seg, n):
    return jax.ops.segment_sum(src, seg, n)
kernel_name = 'mk_vit_tower_d1_tok_img2048_r4_c12fca'

def setup_inputs(seed: int=0):
    np.random.seed(seed)
    _w = jnp.asarray

    def _rec_inputs():
        import jax
        import jax.numpy as jnp
        _rk = jax.random.key(seed)
        x = -0.00340659 + 1.00146 * jax.random.normal(jax.random.fold_in(_rk, 1), (8, 256, 64, 2), jnp.float32)
        return x
    x = _rec_inputs()

    def _L0_tok_setup():
        import jax, jax.numpy as jnp
        import numpy as np
        CH, H, N, N_SSM, SEQ_L = (1, 256, 64, 256, 512)

        def _kernel(C_ri, log_dt, B_ri, inv_A_real, A_imag, L):
            C = C_ri[..., 0] + 1j * C_ri[..., 1]
            B = B_ri[..., 0] + 1j * B_ri[..., 1]
            A = -jnp.exp(inv_A_real) + 1j * A_imag
            rep = log_dt.shape[0] // inv_A_real.shape[0]
            B = jnp.tile(B, (rep, 1))
            A = jnp.tile(A, (rep, 1))
            dt = jnp.exp(log_dt)
            dtA = A * dt[:, None]
            Ct = B[None] * C / (1.0 - dtA / 2) * dt[:, None]
            dA = (1.0 + dtA / 2) / (1.0 - dtA / 2)
            dA_log = jnp.log(dA)
            l = jnp.arange(L, dtype=jnp.float32)
            V = jnp.exp(dA_log[:, :, None] * l)
            K = 2.0 * jnp.einsum('chn,hnl->chl', Ct, V).real
            return K
        key = jax.random.key(seed)
        ks = jax.random.split(key, 5)
        return {'C_ri': jax.random.normal(ks[0], (CH, H, N, 2), dtype=jnp.float32), 'log_dt': jax.random.normal(ks[1], (H,), dtype=jnp.float32), 'B_ri': jax.random.normal(ks[2], (N_SSM, N, 2), dtype=jnp.float32), 'inv_A_real': jax.random.normal(ks[3], (N_SSM, N), dtype=jnp.float32), 'A_imag': jax.random.normal(ks[4], (N_SSM, N), dtype=jnp.float32), 'L': SEQ_L}
    _L0_tok_all = _L0_tok_setup()
    _L0_tok_in = {k: v for k, v in _L0_tok_all.items() if k in ('log_dt', 'B_ri', 'inv_A_real', 'A_imag')}
    del _L0_tok_all

    def _L0_attn_setup():
        import jax, jax.numpy as jnp
        import numpy as np
        D_MODEL = 512
        D_STATE = 64
        D_HEAD = 64
        EXPAND = 2
        CHUNK = 64
        D_INNER = EXPAND * D_MODEL
        N_HEADS = D_INNER // D_HEAD
        PARAM_DIM = 1 + 2 * D_STATE

        def _ssd(a, Bm, Cm, X, Q):
            nb, l = a.shape
            ds = Bm.shape[-1]
            dh = X.shape[-1]
            nc = l // Q
            la = jnp.log(a).reshape(nb, nc, Q)
            cs = jnp.cumsum(la, axis=-1)
            Bc = Bm.reshape(nb, nc, Q, ds)
            Cc = Cm.reshape(nb, nc, Q, ds)
            Xc = X.reshape(nb, nc, Q, dh)
            tri = jnp.tril(jnp.ones((Q, Q), bool))
            L = jnp.where(tri, jnp.exp(cs[..., :, None] - cs[..., None, :]), 0.0)
            scores = jnp.einsum('znid,znjd->znij', Cc, Bc) * L
            y_diag = jnp.einsum('znij,znjh->znih', scores, Xc)
            decay_states = jnp.exp(cs[..., -1:] - cs)
            states = jnp.einsum('znj,znjd,znjh->zndh', decay_states, Bc, Xc)
            A_chunk = jnp.exp(cs[..., -1])

            def step(S, inp):
                Ac, st = inp
                S_prev = S
                return (Ac[:, None, None] * S + st, S_prev)
            S0 = jnp.zeros((nb, ds, dh), a.dtype)
            _, S_prev = jax.lax.scan(step, S0, (A_chunk.T, jnp.moveaxis(states, 1, 0)))
            S_prev = jnp.moveaxis(S_prev, 0, 1)
            y_inter = jnp.einsum('znid,zndh,zni->znih', Cc, S_prev, jnp.exp(cs))
            return (y_diag + y_inter).reshape(nb, l, dh)
        key = jax.random.key(seed)
        k0, k1, k2, k3 = jax.random.split(key, 4)
        x = jax.random.normal(k0, (1, 1024, D_MODEL), jnp.float32)
        w_in = jax.random.normal(k1, (2 * D_INNER, D_MODEL), jnp.float32) * 0.02
        w_param = jax.random.normal(k2, (N_HEADS * PARAM_DIM, D_MODEL), jnp.float32) * 0.02
        w_out = jax.random.normal(k3, (D_MODEL, D_INNER), jnp.float32) * 0.02
        return {'x': x, 'w_in': w_in, 'w_param': w_param, 'w_out': w_out}
    _L0_attn_all = _L0_attn_setup()
    _L0_attn_in = {k: v for k, v in _L0_attn_all.items() if k in ('w_in', 'w_param', 'w_out')}
    del _L0_attn_all

    def _L0_ffn_setup():
        import jax, jax.numpy as jnp
        import numpy as np
        D = 512
        M = 256
        E = 32
        K = 6
        G = 8
        KG = 4
        SH = 512
        SCALE = 2.5

        def _route(xf, Wr, br):
            T = xf.shape[0]
            s = jax.nn.sigmoid(xf @ Wr.T + br)
            sg = s.reshape(T, G, E // G)
            group_w = jax.lax.top_k(sg, 2)[0].sum(-1)
            top_g = jax.lax.top_k(group_w, KG)[1]
            gmask = jnp.zeros((T, G), bool).at[jnp.arange(T)[:, None], top_g].set(True)
            masked = jnp.where(gmask[:, :, None], sg, 0.0).reshape(T, E)
            idx = jax.lax.top_k(masked, K)[1]
            w = jnp.take_along_axis(s, idx, axis=1)
            w = w / (w.sum(-1, keepdims=True) + 1e-20)
            return (idx, w * SCALE)
        key = jax.random.key(seed)
        ks = jax.random.split(key, 7)
        w = 0.02
        return {'hidden_tensor': jax.random.normal(ks[0], (2, 512, D), dtype=jnp.float32), 'Wr': jax.random.normal(ks[1], (E, D), dtype=jnp.float32) * w, 'br': jax.random.normal(ks[2], (E,), dtype=jnp.float32) * w, 'W1': jax.random.normal(ks[3], (E, M, D), dtype=jnp.float32) * w, 'W2': jax.random.normal(ks[4], (E, D, M), dtype=jnp.float32) * w, 'Ws1': jax.random.normal(ks[5], (SH, D), dtype=jnp.float32) * w, 'Ws2': jax.random.normal(ks[6], (D, SH), dtype=jnp.float32) * w}
    _L0_ffn_all = _L0_ffn_setup()
    _L0_ffn_in = {k: v for k, v in _L0_ffn_all.items() if k in ('Wr', 'br', 'W1', 'W2', 'Ws1', 'Ws2')}
    del _L0_ffn_all
    return {'x': x, 'L0_tok_log_dt': _L0_tok_in['log_dt'], 'L0_tok_B_ri': _L0_tok_in['B_ri'], 'L0_tok_inv_A_real': _L0_tok_in['inv_A_real'], 'L0_tok_A_imag': _L0_tok_in['A_imag'], 'L0_attn_w_in': _L0_attn_in['w_in'], 'L0_attn_w_param': _L0_attn_in['w_param'], 'L0_attn_w_out': _L0_attn_in['w_out'], 'L0_ffn_Wr': _L0_ffn_in['Wr'], 'L0_ffn_br': _L0_ffn_in['br'], 'L0_ffn_W1': _L0_ffn_in['W1'], 'L0_ffn_W2': _L0_ffn_in['W2'], 'L0_ffn_Ws1': _L0_ffn_in['Ws1'], 'L0_ffn_Ws2': _L0_ffn_in['Ws2']}

def reference(x, L0_tok_log_dt, L0_tok_B_ri, L0_tok_inv_A_real, L0_tok_A_imag, L0_attn_w_in, L0_attn_w_param, L0_attn_w_out, L0_ffn_Wr, L0_ffn_br, L0_ffn_W1, L0_ffn_W2, L0_ffn_Ws1, L0_ffn_Ws2):
    import jax
    import jax.numpy as jnp

    def _L0_tok_ref(C_ri, log_dt, B_ri, inv_A_real, A_imag, L):
        import jax, jax.numpy as jnp
        import numpy as np
        CH, H, N, N_SSM, SEQ_L = (1, 256, 64, 256, 512)

        def _kernel(C_ri, log_dt, B_ri, inv_A_real, A_imag, L):
            C = C_ri[..., 0] + 1j * C_ri[..., 1]
            B = B_ri[..., 0] + 1j * B_ri[..., 1]
            A = -jnp.exp(inv_A_real) + 1j * A_imag
            rep = log_dt.shape[0] // inv_A_real.shape[0]
            B = jnp.tile(B, (rep, 1))
            A = jnp.tile(A, (rep, 1))
            dt = jnp.exp(log_dt)
            dtA = A * dt[:, None]
            Ct = B[None] * C / (1.0 - dtA / 2) * dt[:, None]
            dA = (1.0 + dtA / 2) / (1.0 - dtA / 2)
            dA_log = jnp.log(dA)
            l = jnp.arange(L, dtype=jnp.float32)
            V = jnp.exp(dA_log[:, :, None] * l)
            K = 2.0 * jnp.einsum('chn,hnl->chl', Ct, V).real
            return K
        return _kernel(C_ri, log_dt, B_ri, inv_A_real, A_imag, L)

    def _L0_attn_ref(x, w_in, w_param, w_out):
        import jax, jax.numpy as jnp
        import numpy as np
        D_MODEL = 512
        D_STATE = 64
        D_HEAD = 64
        EXPAND = 2
        CHUNK = 64
        D_INNER = EXPAND * D_MODEL
        N_HEADS = D_INNER // D_HEAD
        PARAM_DIM = 1 + 2 * D_STATE

        def _ssd(a, Bm, Cm, X, Q):
            nb, l = a.shape
            ds = Bm.shape[-1]
            dh = X.shape[-1]
            nc = l // Q
            la = jnp.log(a).reshape(nb, nc, Q)
            cs = jnp.cumsum(la, axis=-1)
            Bc = Bm.reshape(nb, nc, Q, ds)
            Cc = Cm.reshape(nb, nc, Q, ds)
            Xc = X.reshape(nb, nc, Q, dh)
            tri = jnp.tril(jnp.ones((Q, Q), bool))
            L = jnp.where(tri, jnp.exp(cs[..., :, None] - cs[..., None, :]), 0.0)
            scores = jnp.einsum('znid,znjd->znij', Cc, Bc) * L
            y_diag = jnp.einsum('znij,znjh->znih', scores, Xc)
            decay_states = jnp.exp(cs[..., -1:] - cs)
            states = jnp.einsum('znj,znjd,znjh->zndh', decay_states, Bc, Xc)
            A_chunk = jnp.exp(cs[..., -1])

            def step(S, inp):
                Ac, st = inp
                S_prev = S
                return (Ac[:, None, None] * S + st, S_prev)
            S0 = jnp.zeros((nb, ds, dh), a.dtype)
            _, S_prev = jax.lax.scan(step, S0, (A_chunk.T, jnp.moveaxis(states, 1, 0)))
            S_prev = jnp.moveaxis(S_prev, 0, 1)
            y_inter = jnp.einsum('znid,zndh,zni->znih', Cc, S_prev, jnp.exp(cs))
            return (y_diag + y_inter).reshape(nb, l, dh)
        b, l, _ = x.shape
        xr = x @ w_in.T
        inp, res = (xr[..., :D_INNER], xr[..., D_INNER:])
        params = (x @ w_param.T).reshape(b, l, N_HEADS, PARAM_DIM)
        dt = jax.nn.softplus(params[..., 0])
        a = jnp.exp(-dt)
        Bp = params[..., 1:1 + D_STATE]
        Cp = params[..., 1 + D_STATE:]
        nb = b * N_HEADS
        y = _ssd(a.reshape(nb, l), Bp.reshape(nb, l, D_STATE), Cp.reshape(nb, l, D_STATE), inp.reshape(nb, l, D_HEAD), CHUNK)
        y = y.reshape(b, l, D_INNER)
        out = y * jax.nn.silu(res)
        return out @ w_out.T

    def _L0_ffn_ref(hidden_tensor, Wr, br, W1, W2, Ws1, Ws2):
        import jax, jax.numpy as jnp
        import numpy as np
        D = 512
        M = 256
        E = 32
        K = 6
        G = 8
        KG = 4
        SH = 512
        SCALE = 2.5

        def _route(xf, Wr, br):
            T = xf.shape[0]
            s = jax.nn.sigmoid(xf @ Wr.T + br)
            sg = s.reshape(T, G, E // G)
            group_w = jax.lax.top_k(sg, 2)[0].sum(-1)
            top_g = jax.lax.top_k(group_w, KG)[1]
            gmask = jnp.zeros((T, G), bool).at[jnp.arange(T)[:, None], top_g].set(True)
            masked = jnp.where(gmask[:, :, None], sg, 0.0).reshape(T, E)
            idx = jax.lax.top_k(masked, K)[1]
            w = jnp.take_along_axis(s, idx, axis=1)
            w = w / (w.sum(-1, keepdims=True) + 1e-20)
            return (idx, w * SCALE)
        B, Tlen, C = hidden_tensor.shape
        xf = hidden_tensor.reshape(-1, C).astype(jnp.float32)
        T = xf.shape[0]
        idx, w = _route(xf, Wr, br)
        gate = jnp.zeros((T, E), w.dtype).at[jnp.arange(T)[:, None], idx].add(w)

        def step(acc, ew):
            w1, w2, g = ew
            h = jnp.square(jax.nn.relu(xf @ w1.T)) @ w2.T
            return (acc + g[:, None] * h, None)
        acc, _ = jax.lax.scan(step, jnp.zeros_like(xf), (W1, W2, gate.T))
        moe_out = acc.reshape(B, Tlen, C).astype(hidden_tensor.dtype)
        shared = jnp.square(jax.nn.relu(hidden_tensor @ Ws1.T)) @ Ws2.T
        return shared + moe_out
    h = _L0_tok_ref(x, L0_tok_log_dt, L0_tok_B_ri, L0_tok_inv_A_real, L0_tok_A_imag, 512)
    h = h + _L0_attn_ref(_layernorm(h, axis=-1), L0_attn_w_in, L0_attn_w_param, L0_attn_w_out)
    h = h + _L0_ffn_ref(_layernorm(h, axis=-1), L0_ffn_Wr, L0_ffn_br, L0_ffn_W1, L0_ffn_W2, L0_ffn_Ws1, L0_ffn_Ws2)
    return h

_drawn_inputs = setup_inputs


def setup_inputs(seed=0):
    import zlib

    import numpy as np

    out = dict(_drawn_inputs(seed))
    spreads = {}
    factors = {'L0_ffn_br': 3.858}
    for name, (base, spread) in spreads.items():
        noise = np.random.default_rng([zlib.crc32(name.encode()), seed]).standard_normal(out[name].shape)
        drawn = base * np.exp(spread * noise) if base else spread * noise
        out[name] = jnp.asarray(drawn.astype(out[name].dtype))
    for name, factor in factors.items():
        out[name] = (out[name] * factor).astype(out[name].dtype)
    return out
```

```python
import numpy as np
import concourse.bass as bass
from concourse import mybir
from contextlib import ExitStack

F32 = mybir.dt.float32
I32 = mybir.dt.int32
U32 = mybir.dt.uint32
ALU = mybir.AluOpType
ACT = mybir.ActivationFunctionType
AX = mybir.AxisListType

P = 128
NB, NH, D = 8, 256, 512
NT = NB * NH // P
J = 8
HEADS, DS, DH = 16, 64, 64
NCK = 16
KT = D // P
EXP, MH, TOPK, GROUPS, GTOP = 32, 256, 6, 8, 4
GSZ = EXP // GROUPS
SCALE = 2.5
EPS = 1e-5
CAP = NT * P + P


def wait_alone(engine, sem, value, counted):
    engine.wait_ge(sem, value)
    if not isinstance(value, int):
        engine.sem_inc(counted, 1)


class Steps:

    def __init__(self, engine, sem, per_tile=0, counted=None):
        self.engine, self.sem, self.per_tile, self.counted = engine, sem, per_tile, counted
        self.base, self.n = 0, 0

    def start(self, tile):
        self.base, self.n = tile * self.per_tile, 0

    def link(self, instruction, alone=False):
        self.n += 1
        instruction.then_inc(self.sem, 1)
        if alone:
            wait_alone(self.engine, self.sem, self.base + self.n, self.counted)
        else:
            self.engine.wait_ge(self.sem, self.base + self.n)

    def end(self):
        assert self.n == self.per_tile, (self.n, self.per_tile)


def build(nc, t):
    ctx = ExitStack()
    with ctx:

        def sb(name, shape, dt=F32):
            return ctx.enter_context(nc.sbuf_tensor(name, shape, dt))

        def sem(name):
            return ctx.enter_context(nc.semaphore(name))

        w_bx = sb("w_bx", [P, KT, HEADS * P])
        w_c = sb("w_c", [P, KT, HEADS * DS])
        w_r = sb("w_r", [P, KT, HEADS * DH])
        w_dt = sb("w_dt", [P, KT, P])
        w_o = sb("w_o", [P, 8, D])
        w_s1 = sb("w_s1", [P, KT, D])
        w_s2 = sb("w_s2", [P, KT, D])
        w_rt = sb("w_rt", [P, KT, EXP])
        brow = sb("brow", [P, EXP])
        ident = sb("ident", [P, P])
        m_gt = sb("m_gt", [P, P])
        m_le = sb("m_le", [P, P])
        m_lt = sb("m_lt", [P, P])
        ones = sb("ones", [P, P])
        diag = sb("diag", [P, J])
        iota = sb("iota", [P, EXP])
        z8 = sb("z8", [P, 6, P])
        v4 = sb("v4", [P, 2, P, 8])
        z64 = sb("z64", [P, 2, P, 8])
        q = sb("q", [P, 2, P])
        c_in = sb("c_in", [P, 2, J * NB])
        vz = sb("vz", [P, 2, J, 64])
        wd = sb("wd", [P, 2, J, 2, 2, 32])
        w0 = sb("w0", [P, 2, J, NB])
        tp = sb("tp", [P, 2, J * 64])
        tv = sb("tv", [P, 1024])
        xT = sb("xT", [P, KT, P])
        h_new = sb("h_new", [P, D])
        h_cur = sb("h_cur", [P, D])
        h2 = sb("h2", [P, D])
        xn = sb("xn", [P, D])
        xn2 = sb("xn2", [P, D])
        x2T = sb("x2T", [P, KT, P])
        bx = sb("bx", [P, P * HEADS])
        ct = sb("ct", [DS, P * HEADS])
        gt = sb("gt", [P, 8, P])
        rd = sb("rd", [P, NCK, P])
        e0 = sb("e0", [DS, NB, P])
        xp = sb("xp", [P, NCK, DH])
        bd = sb("bd", [P, NB, DS])
        st = sb("st", [DS, NB, DH])
        us = sb("us", [P, KT, P])
        dr = sb("dr", [P, 4, NCK])
        dcy = sb("dcy", [P, NCK])
        bn = sb("bn", [P, 2, 6])
        mv = sb("mv", [P, 2, 2])
        rs = sb("rs", [P, 2])
        var = sb("var", [P, 2, 2])
        s_rt = sb("s_rt", [P, 3, EXP])
        oh = sb("oh", [P, 2, TOPK, EXP])
        gp = sb("gp", [P, 9, GROUPS])
        gsum = sb("gsum", [P, 4])
        gix = sb("gix", [P, 8], U32)
        top = sb("top", [P, 8])
        tix = sb("tix", [P, 8], U32)
        tixf = sb("tixf", [P, 2, 8])
        msk = sb("msk", [P, EXP])
        macc = sb("macc", [P, EXP])
        posf = sb("posf", [P, 8])
        table = sb("table", [1, 2 * EXP + 2 * EXP * NT], I32)
        behind = sb("behind", [P, EXP])
        pick = sb("pick", [P, 2, TOPK], U32)
        gnow = sb("gnow", [P, 2, TOPK])
        slot_now = sb("slot_now", [P, TOPK], U32)
        chosen = sb("chosen", [P, NT, 8])
        place_in = sb("place_in", [P, NT, 8])
        gate = sb("gate", [P, NT, 8])

        bank = [ctx.enter_context(nc.psum_tensor(f"bank{i}", [P, 512], F32)) for i in range(8)]

        lists = nc.dram_tensor("expert_rows", [EXP * CAP, D], F32, kind="Internal").ap()
        results = nc.dram_tensor("expert_results", [NT * P * TOPK + P, D], F32, kind="Internal").ap()
        h3_dram = nc.dram_tensor("h_and_shared", [NT, P, D], F32, kind="Internal").ap()

        s_pre = sem("s4d_inputs_loaded")
        s_wf = sem("first_weights_loaded")
        s_ws = sem("later_weights_loaded")
        s_cin = sem("c_loaded")
        s_out = sem("out_stored")
        s_h3 = sem("h3_stored")
        s_scat = sem("rows_scattered")
        k_const = sem("constants_ready")
        pool_step = sem("pool_prologue_step")
        dve_pre = sem("dve_prologue_step")
        s_exps = sem("prologue_exps")
        z_ready = sem("z_powers_ready")
        fv_step, fp_step, fa_step = sem("front_dve_step"), sem("front_pool_step"), sem("front_act_step")
        v_ready, w_ready = sem("v_ready"), sem("w_ready")
        hgen_done, hT_ready, htok_done = sem("hgen_done"), sem("hT_ready"), sem("htok_done")
        xn_ready, xnT_done, xnT_ready = sem("xn_ready"), sem("xnT_done"), sem("xnT_ready")
        mv_step, ma_step = sem("main_dve_step"), sem("main_act_step")
        dtraw_done, dtin_ready, sp_ready, dt_ready = (sem(n) for n in ("dtraw_done", "dtin_ready", "sp_ready", "dt_ready"))
        bx_done, bx_copied, c_done, c_copied = (sem(n) for n in ("bx_done", "bx_copied", "c_done", "c_copied"))
        res_done, sigmoid_ready, silu_step, g_ready = (sem(n) for n in ("res_done", "sigmoid_ready", "silu_step", "g_ready"))
        sigma_done, decay_ready, rd_ready = (sem(n) for n in ("sigma_done", "decay_ready", "rd_ready"))
        e0_done, e0_ready, d_done, e_ready, em_ready = (sem(n) for n in ("e0_done", "e0_ready", "d_done", "e_ready", "em_ready"))
        bxtr_done, xp_ready, scores_done, p_ready, cts_ready = (sem(n) for n in ("bxtr_done", "xp_ready", "scores_done", "p_ready", "cts_ready"))
        st_done, st_ready, y_done, yg_ready, out_done, xn2_ready = (sem(n) for n in ("st_done", "st_ready", "y_done", "yg_ready", "out_done", "xn2_ready"))
        tv_step, ta_step = sem("tail_dve_step"), sem("tail_act_step")
        x2T_done, x2T_ready, logits_done, rexp2_ready, lsum_ready = (sem(n) for n in ("x2T_done", "x2T_ready", "logits_done", "router_exp_ready", "logits_ready"))
        up_done, us_ready, down_done, h3_ready = (sem(n) for n in ("up_done", "us_ready", "down_done", "h3_ready"))
        mask_ready, rank_done, slot_ready = (sem(n) for n in ("mask_ready", "rank_done", "slot_ready"))

        out_tiles = [t["out"][c] for c in range(NB)]
        block = ctx.enter_context(nc.Block())


        waited_dve, waited_pool, waited_sp, waited_pe = (sem(n) for n in ("waited_dve", "waited_pool", "waited_sp", "waited_pe"))
        pre = bx[:, 0:5 * P].rearrange("p (k x) -> p k x", k=5)
        tmp = rd[:, :, :].rearrange("p (a b) i -> p a (b i)", a=16)

        ct_hd = ct[:, :].rearrange("p (t q par) -> p t q par", q=8, par=2)
        ct_ck = ct[:, :].rearrange("p (c hh i) -> p c hh i", c=NB, hh=2)
        bx_hd = bx[:, :].rearrange("p (t h) -> p t h", h=HEADS)
        bx_ck = bx[:, :].rearrange("p (k i) -> p k i", i=P)
        rd_half = rd[:, :, :].rearrange("p (c hh) i -> p c hh i", hh=2)

        WB = 4
        w_exp = [w_bx[:, 0, :], w_bx[:, 1, :]]
        w_exp += [w_o[:, 4 * i:4 * i + 4, :].rearrange("p k d -> p (k d)") for i in range(2)]
        w1 = [w_exp[par][:, 0:KT * MH].rearrange("p (k m) -> p k m", k=KT) for par in range(WB)]
        w2 = [w_exp[par][:, KT * MH:].rearrange("p (k d) -> p k d", k=MH // P) for par in range(WB)]
        x_ring, y_ring = w_bx[:, 2, :], w_bx[:, 3, :]
        xs, xsT, hu = xn[:, :], xT, us[:, 0:2, :]
        comb = [w_c[:, :, :].rearrange("p k n -> p (k n)"), w_r[:, :, :].rearrange("p k n -> p (k n)")]
        zeros_ready, zeros_in = sem("zeros_ready"), sem("zeros_stored")
        counts_done, tiles_ready, table_done, table_ready = (sem(n) for n in ("counts_done", "tiles_ready", "table_done", "table_ready"))
        tb_step = sem("table_step")
        w_first, w_in = sem("first_experts_loaded"), [sem(f"expert_weights_loaded{i}") for i in range(4)]
        x_in, xs_ready, trx_done, xsT_ready = (sem(n) for n in ("x_tile_loaded", "xs_ready", "xs_transposed", "xsT_ready"))
        h_done, relu_step, hu_ready = (sem(n) for n in ("h_done", "relu_step", "hu_ready"))
        y2_done, y_ready, y_out, y_free = (sem(n) for n in ("expert_y_done", "expert_y_ready", "expert_y_stored", "y_slots_freed"))
        gate_ready, pick_step = sem("gates_ready"), sem("pick_step")
        pick_ready, got_h3 = sem("picks_ready"), [sem(f"h3_loaded{i}") for i in range(2)]
        got = [sem(f"results_gathered{i}") for i in range(2)]
        comb_step, o_ready = sem("combine_step"), sem("out_tile_ready")
        o_out = [sem(f"out_tile_stored{i}") for i in range(2)]
        RING = 4

        def expert_of(engine, e):
            return (engine.value_load(table[0:1, bass.ds(e, 1)], min_val=0, max_val=NT * TOPK + EXP),
                    engine.value_load(table[0:1, bass.ds(EXP + e, 1)], min_val=1, max_val=NT))

        def list_row(engine, e, i):
            return engine.value_load(table[0:1, bass.ds(2 * EXP + e * NT + i, 1)], min_val=0, max_val=EXP * CAP - P)

        def result_row(engine, e, i):
            return engine.value_load(table[0:1, bass.ds((2 + NT) * EXP + e * NT + i, 1)], min_val=0, max_val=NT * P * TOPK)

        def slot_of(tile):
            return bass.ds((tile % RING) * D, D)

        @block.sync
        def _(sp):
            sp.dma_start(pre, t["s4d"]).then_inc(s_pre, 16)
            sp.dma_start(c_in[:, :, :], t["c_tiles"][0]).then_inc(s_cin, 16)
            for dst, name in ((w_dt, "w_dt"), (w_bx, "w_bx"), (w_c, "w_c"), (w_r, "w_r")):
                sp.dma_start(dst[:, :, :], t[name]).then_inc(s_wf, 16)
            for dst, name in ((w_o, "w_o"), (w_rt, "w_rt"), (w_s1, "w_s1"), (w_s2, "w_s2")):
                sp.dma_start(dst[:, :, :], t[name]).then_inc(s_ws, 16)
            sp.dma_start(brow[:, :], t["br"]).then_inc(s_ws, 16)

            def load_c(g):
                wait_alone(sp, w_ready, g, waited_sp)
                sp.dma_start(c_in[:, :, :], tile_of(t["c_tiles"], g)).then_inc(s_cin, 16)

            def store_h3(g):
                wait_alone(sp, h3_ready, g + 1, waited_sp)
                sp.dma_start(tile_of(h3_dram, g), h2[:, :]).then_inc(s_h3, 16)

            sp.wait_ge(zeros_ready, 1)
            with sp.Fori(0, EXP) as e:
                sp.dma_start(lists.rearrange("(e r) d -> e r d", e=EXP)[bass.ds(e, 1), 0:P, :].rearrange("o r d -> (o r) d"),
                             x2T[:, :, :].rearrange("p k t -> p (k t)")).then_inc(zeros_in, 16)
            load_c(1)
            load_c(2)
            with sp.Fori(1, NT - 2) as g:
                load_c(g + 2)
                store_h3(g - 1)
            store_h3(NT - 3)
            store_h3(NT - 2)
            sp.wait_ge(res_done, 2 * NT)
            for par in range(WB):
                if par == 2:
                    sp.wait_ge(out_done, NT)
                sp.dma_start(w_exp[par], t["experts"][par]).then_inc(w_first, 16)
            store_h3(NT - 1)

            sp.wait_ge(table_ready, 1)
            sp.wait_ge(s_scat, 16 * TOPK * NT)
            sp.sem_inc(xs_ready, RING)
            sp.sem_inc(x_in, 16)

            def load_x(row, tile):
                wait_alone(sp, xs_ready, tile + 1, waited_sp)
                wait_alone(sp, x_in, 16 * (tile + 1), waited_sp)
                sp.dma_start(x_ring[:, slot_of(tile)], lists[bass.ds(row, P), :]).then_inc(x_in, 16)

            with sp.Fori(0, EXP) as e:
                base, n = expert_of(sp, e)
                with sp.Fori(0, n) as i:
                    load_x(list_row(sp, e, i), base + i)
            base, n = expert_of(sp, EXP - 1)
            load_x(0, sp.snap(base + n))

            sp.wait_ge(s_h3, 16 * NT)

            def load_h3(g, par):
                sp.dma_start(comb[par][:, 6 * D:7 * D], tile_of(h3_dram, g)).then_inc(got_h3[par], 16)

            def store_out(pair, par):
                wait_alone(sp, o_ready, 2 * pair + par + 1, waited_sp)
                for c in range(NB):
                    sp.dma_start(out_tiles[c][bass.ds((2 * pair + par) * 16, 16), :],
                                 comb[par][16 * c:16 * c + 16, 7 * D:8 * D]).then_inc(o_out[par], 16)

            for par in range(2):
                load_h3(par, par)
            with sp.Fori(0, NT // 2 - 1) as pair:
                for par in range(2):
                    store_out(pair, par)
                    load_h3(2 * pair + 2 + par, par)
            for par in range(2):
                store_out(NT // 2 - 1, par)
            for par in range(2):
                sp.wait_ge(o_out[par], 16 * NB * NT // 2)

        @block.gpsimd
        def _(pool):
            step = Steps(pool, pool_step)
            for m in (ident, m_gt, m_le, m_lt, ones):
                pool.memset(m[:, :], 0.0 if m is ident else 1.0)
            pool.memset(diag[:, :], 1.0)
            pool.memset(macc[:, :], 0.0)
            pool.iota(iota[:, :], pattern=[[1, EXP]], base=0, channel_multiplier=0,
                      allow_small_or_imprecise_dtypes=True)
            step.link(pool.memset(wd[:, :, :, :, :, :], 0.0))
            pool.affine_select(out=ident[:, :], in_=ident[:, :], compare_op=ALU.not_equal, fill=1.0,
                               base=0, pattern=[[-1, P]], channel_multiplier=1)
            pool.affine_select(out=m_gt[:, :], in_=m_gt[:, :], compare_op=ALU.is_gt, fill=0.0,
                               base=0, pattern=[[-1, P]], channel_multiplier=1)
            pool.affine_select(out=m_le[:, :], in_=m_le[:, :], compare_op=ALU.is_ge, fill=0.0,
                               base=0, pattern=[[1, P]], channel_multiplier=-1)
            pool.affine_select(out=m_lt[:, :], in_=m_lt[:, :], compare_op=ALU.is_gt, fill=0.0,
                               base=0, pattern=[[1, P]], channel_multiplier=-1)
            step.link(pool.affine_select(out=diag[:, :], in_=diag[:, :], compare_op=ALU.is_ge, fill=0.0,
                                         base=0, pattern=[[-HEADS, J]], channel_multiplier=1))
            pool.affine_select(out=diag[:, :], in_=diag[:, :], compare_op=ALU.is_gt, fill=0.0,
                               base=HEADS, pattern=[[HEADS, J]], channel_multiplier=-1).then_inc(k_const, 1)

            def front(g):
                fs = Steps(pool, fp_step, 7, waited_pool)
                fs.start(g)
                pool.wait_ge(s_cin, (g + 1) * 16)
                if not (isinstance(g, int) and g == 0):
                    wait_alone(pool, hgen_done, g, waited_pool)
                C = lambda i: c_in[:, i, :].rearrange("p (j c) -> p j c", j=J)
                Q = lambda i: q[:, i, bass.ds(g * J, J)].unsqueeze(2).broadcast_to([P, J, NB])
                T8 = lambda i: tp[:, i, 0:J * NB].rearrange("p (j c) -> p j c", j=J)
                pool.tensor_tensor(T8(0), C(0), Q(0), ALU.mult)
                fs.link(pool.tensor_tensor(T8(1), C(1), Q(1), ALU.mult))
                fs.link(pool.tensor_tensor(w0[:, 0, :, :], T8(0), T8(1), ALU.add), alone=True)
                pool.tensor_tensor(T8(0), C(0), Q(1), ALU.mult)
                fs.link(pool.tensor_tensor(T8(1), C(1), Q(0), ALU.mult))
                fs.link(pool.tensor_tensor(w0[:, 1, :, :], T8(0), T8(1), ALU.subtract), alone=True)
                W = lambda i: w0[:, i, :, :].unsqueeze(3).broadcast_to([P, J, NB, 8])
                Z = lambda i: z64[:, i, bass.ds(g * J, J), :].unsqueeze(2).broadcast_to([P, J, NB, 8])
                T = lambda i: tp[:, i, :].rearrange("p (j c a) -> p j c a", j=J, c=NB)
                for i, (za, zb, op) in enumerate(((0, 1, ALU.subtract), (1, 0, ALU.add))):
                    pool.tensor_tensor(T(0), W(0), Z(za), ALU.mult)
                    fs.link(pool.tensor_tensor(T(1), W(1), Z(zb), ALU.mult))
                    for hh in range(2):
                        lanes = slice(64 * hh, 64 * hh + 64)
                        V = lambda k: tp[lanes, k, :].rearrange("p (j m par) -> p j par m", j=J, par=2)
                        last = pool.tensor_tensor(wd[lanes, i, :, hh, :, :], V(0), V(1), op)
                    if i == 0:
                        fs.link(last, alone=True)
                fs.end()
                last.then_inc(w_ready, 1)
                pool.wait_ge(w_ready, g + 1)

            def dt_tri(g):
                pool.wait_ge(dt_ready, g + 1)
                if not (isinstance(g, int) and g == 0):
                    pool.wait_ge(y_done, 2 * g)
                pool.tensor_tensor(rd[:, :, :], m_le[:, :].unsqueeze(1).broadcast_to([P, NCK, P]),
                                   dr[:, 3, :].unsqueeze(2).broadcast_to([P, NCK, P]), ALU.mult).then_inc(rd_ready, 1)

            def causal(g):
                for k in range(4):
                    wait_alone(pool, e_ready, 4 * g + k + 1, waited_pool)
                    part = rd[:, 4 * k:4 * k + 4, :]
                    pool.affine_select(out=part, in_=part, compare_op=ALU.is_ge, fill=0.0, base=0,
                                       pattern=[[0, 4], [1, P]], channel_multiplier=-1).then_inc(em_ready, 1)

            def scatter(g):
                wait_alone(pool, slot_ready, g + 1, waited_pool)
                for k in range(TOPK):
                    pool.indirect_dma_start(
                        out=lists, out_offset=bass.IndirectOffsetOnAxis(ap=slot_now[:, k:k + 1], axis=0),
                        in_=xn2[:, :], in_offset=None).then_inc(s_scat, 16)
                pool.wait_ge(s_scat, 16 * TOPK * (g + 1))

            pool.wait_ge(z_ready, 1)
            front(0)

            def iteration(g, first=False, last=False):
                if not last:
                    front(g + 1)
                dt_tri(g)
                causal(g)
                if not first:
                    scatter(g - 1)

            iteration(0, first=True)
            pool.wait_ge(zeros_in, 16 * EXP)
            with pool.Fori(1, NT - 1) as g:
                iteration(g)
            iteration(NT - 1, last=True)
            scatter(NT - 1)

            pool.wait_ge(table_ready, 1)
            pool.sem_inc(y_free, RING)

            def store_y(e, i, tile):
                row = result_row(pool, e, i)
                wait_alone(pool, y_ready, tile + 2, waited_pool)
                pool.dma_start(results[bass.ds(row, P), :], y_ring[:, slot_of(tile)]).then_inc(y_out, 16)
                wait_alone(pool, y_out, 16 * (tile + 1), waited_pool)
                pool.sem_inc(y_free, 1)

            with pool.Fori(0, EXP // WB - 1) as four:
                for par in range(WB):
                    e = WB * four + par
                    base, n = expert_of(pool, e)
                    with pool.Fori(0, n) as i:
                        store_y(e, i, base + i)
                    pool.dma_start(w_exp[par], t["experts"][bass.ds(e + WB, 1)].rearrange("o p n -> (o p) n")).then_inc(w_in[par], 16)
            with pool.Fori(EXP - WB, EXP) as e:
                base, n = expert_of(pool, e)
                with pool.Fori(0, n) as i:
                    store_y(e, i, base + i)

            def gather(pair, par):
                wait_alone(pool, pick_ready, 2 * pair + par + 1, waited_pool)
                for k in range(TOPK):
                    pool.indirect_dma_start(out=comb[par][:, D * k:D * k + D], out_offset=None, in_=results[0:NT * P * TOPK, :],
                                            in_offset=bass.IndirectOffsetOnAxis(ap=pick[:, par, k:k + 1], axis=0)).then_inc(got[par], 16)

            with pool.Fori(0, NT // 2) as pair:
                for par in range(2):
                    gather(pair, par)

        @block.scalar
        def _(act):
            nc.scalar.preload_act_table_set("natural_log_exp_and_others")
            act.wait_ge(s_pre, 16)
            act.activation(tmp[:, 0, :], pre[:, 0, :], ACT.Exp)
            act.activation(tmp[:, 1, :], pre[:, 2, :], ACT.Exp).then_inc(s_exps, 1)

            def front_h(g):
                act.wait_ge(hgen_done, g + 1)
                src = bank[6][:, :].rearrange("p (j hh c a) -> p j hh c a", j=J, hh=2, c=NB)
                for hh in range(2):
                    for a in range(KT):
                        last = act.activation(xT[:, a, :].rearrange("p (c hh j) -> p hh c j", hh=2, j=J)[:, hh],
                                              src[:, :, hh, :, a].rearrange("p j c -> p c j"), ACT.Copy)
                last.then_inc(hT_ready, 1)

            def front_x(g):
                act.wait_ge(xnT_done, g + 1)
                act.activation(xT[:, :, :], bank[6][:, :].rearrange("p (k t) -> p k t", k=KT), ACT.Copy).then_inc(xnT_ready, 1)

            def copy_bx(g, k):
                act.wait_ge(bx_done, 4 * g + k + 1)
                act.activation(bx_hd[:, :, 4 * k:4 * k + 4], bank[1 + k % 2][:, :].rearrange("p (h t) -> p t h", h=4),
                               ACT.Copy).then_inc(bx_copied, 1)

            def main(g, tail):
                ms = Steps(act, ma_step, 1)
                ms.start(g)
                copy_bx(g, 0)
                act.wait_ge(dtin_ready, g + 1)
                ms.link(act.activation(dr[:, 2, :], dr[:, 1, :], ACT.Exp))
                act.activation(dr[:, 2, :], dr[:, 2, :], ACT.Ln, bias=1.0).then_inc(sp_ready, 1)
                ms.end()
                for k in range(1, 4):
                    copy_bx(g, k)
                for b in range(2):
                    act.wait_ge(c_done, 2 * g + b + 1)
                    for par in range(2):
                        last = act.activation(ct_hd[:, :, 4 * b:4 * b + 4, par],
                                              bank[1 + b][64 * par:64 * par + 64, :].rearrange("p (q t) -> p t q", q=4), ACT.Copy)
                    last.then_inc(c_copied, 1)
                if tail:
                    act.wait_ge(x2T_done, g)
                    act.activation(x2T[:, :, :], bank[3][:, :].rearrange("p (k t) -> p k t", k=KT), ACT.Copy).then_inc(x2T_ready, 1)
                ss = Steps(act, silu_step, 4)
                ss.start(g)
                for b in range(2):
                    act.wait_ge(res_done, 2 * g + b + 1)
                    part = gt[:, 4 * b:4 * b + 4, :]
                    ss.link(act.activation(part, bank[1 + b][:, :].rearrange("p (q t) -> p q t", q=4), ACT.Exp, scale=-1.0))
                    ss.link(act.activation(part, part, ACT.Ln, bias=1.0))
                    act.activation(part, part, ACT.Exp, scale=-1.0).then_inc(sigmoid_ready, 1)
                ss.end()
                if tail:
                    tail_a(g - 1)
                act.wait_ge(sigma_done, g + 1)
                act.activation(dcy[:, :], bank[0][:, 0:NCK], ACT.Exp, scale=-1.0).then_inc(decay_ready, 1)
                for b in range(2):
                    act.wait_ge(e0_done, 2 * g + b + 1)
                    act.activation(e0[:, 4 * b:4 * b + 4, :], bank[4 + b][0:DS, :].rearrange("p (c i) -> p c i", c=4),
                                   ACT.Exp, scale=-1.0).then_inc(e0_ready, 1)
                for k in range(4):
                    act.wait_ge(d_done, 4 * g + k + 1)
                    act.activation(rd[:, 4 * k:4 * k + 4, :], bank[4 + k % 2][:, :].rearrange("p (c i) -> p c i", c=4),
                                   ACT.Exp, scale=-1.0).then_inc(e_ready, 1)

            def tail_a(g):
                act.wait_ge(lsum_ready, g + 1)
                act.activation(s_rt[:, 1, :], s_rt[:, 0, :], ACT.Exp, scale=-1.0).then_inc(rexp2_ready, 1)
                act.wait_ge(up_done, g + 1)
                ts = Steps(act, ta_step, 1)
                ts.start(g)
                ts.link(act.activation(us[:, :, :], bank[3][:, :].rearrange("p (k t) -> p k t", k=KT), ACT.Relu))
                ts.end()
                act.activation(us[:, :, :], us[:, :, :], ACT.Square).then_inc(us_ready, 1)

            def copy_st(g):
                act.wait_ge(st_done, g + 1)
                act.activation(st[:, :, :], bank[0][0:DS, :].rearrange("p (c h) -> p c h", c=NB), ACT.Copy).then_inc(st_ready, 1)

            front_h(0)
            front_x(0)

            def iteration(g, first=False, last=False):
                main(g, not first)
                if not last:
                    front_h(g + 1)
                copy_st(g)
                if not last:
                    front_x(g + 1)

            iteration(0, first=True)
            act.wait_ge(zeros_in, 16 * EXP)
            with act.Fori(1, NT - 1) as g:
                iteration(g)
            iteration(NT - 1, last=True)
            act.wait_ge(x2T_done, NT)
            act.activation(x2T[:, :, :], bank[3][:, :].rearrange("p (k t) -> p k t", k=KT), ACT.Copy).then_inc(x2T_ready, 1)
            tail_a(NT - 1)

            def copy_x(tile):
                act.wait_ge(trx_done, tile + 1)
                act.activation(xsT[:, :, :], bank[2][:, :].rearrange("p (k t) -> p k t", k=KT), ACT.Copy).then_inc(xsT_ready, 1)

            act.wait_ge(table_ready, 1)
            copy_x(0)
            with act.Fori(0, EXP) as e:
                base, n = expert_of(act, e)
                with act.Fori(0, n) as i:
                    tile = act.snap(base + i)
                    for m in range(2):
                        act.wait_ge(h_done, 2 * tile + m + 1)
                        act.activation(hu[:, m, :], bank[m][:, 0:P], ACT.Relu).then_inc(relu_step, 1)
                        act.wait_ge(relu_step, 2 * tile + m + 1)
                        act.activation(hu[:, m, :], hu[:, m, :], ACT.Square).then_inc(hu_ready, 1)
                    copy_x(tile + 1)

        @block.vector
        def _(dve):
            step = Steps(dve, dve_pre)
            L = step.link
            tt, ts_, stt = dve.tensor_tensor, dve.tensor_scalar, dve.scalar_tensor_tensor
            dve.wait_ge(s_pre, 16)
            dve.wait_ge(s_exps, 1)
            T = lambda i: tmp[:, i, :]
            nega, dt, ur, ui, t2, t3, n_, om, den = (T(i) for i in range(9))
            A_im, Br, Bi = pre[:, 1, :], pre[:, 3, :], pre[:, 4, :]
            L(stt(ur, nega, -0.5, dt, ALU.mult, ALU.mult))
            L(stt(ui, A_im, 0.5, dt, ALU.mult, ALU.mult))
            L(tt(t2, ui, ui, ALU.mult))
            L(tt(t3, ur, ur, ALU.mult))
            L(ts_(om, ur, -1.0, 1.0, ALU.mult, ALU.add))
            L(tt(n_, t2, t3, ALU.add))
            L(tt(den, om, om, ALU.mult))
            L(tt(den, den, t2, ALU.add))
            L(dve.reciprocal(den, den))
            L(ts_(n_, n_, -1.0, 1.0, ALU.mult, ALU.add))
            v = lambda i, b: v4[:, i, :, b]
            dve.memset(v4[:, 0, :, 0], 1.0)
            dve.memset(v4[:, 1, :, 0], 0.0)
            dve.memset(z64[:, 0, :, 0], 1.0)
            dve.memset(z64[:, 1, :, 0], 0.0)
            L(tt(v(0, 1), n_, den, ALU.mult))
            L(stt(v(1, 1), ui, 2.0, den, ALU.mult, ALU.mult))
            L(stt(t3, dt, 2.0, den, ALU.mult, ALU.mult))
            L(tt(t2, Br, om, ALU.mult))
            L(tt(n_, Bi, ui, ALU.mult))
            L(tt(t2, t2, n_, ALU.subtract))
            L(tt(q[:, 0, :], t2, t3, ALU.mult))
            L(tt(t2, Br, ui, ALU.mult))
            L(tt(n_, Bi, om, ALU.mult))
            L(tt(t2, t2, n_, ALU.add))
            L(stt(q[:, 1, :], t2, -1.0, t3, ALU.mult, ALU.mult))

            def cmul(link, o, a, b, s, minus=False):
                tt(s[0], a[0], b[0], ALU.mult)
                tt(s[1], a[1], b[1], ALU.mult)
                tt(s[2], a[0], b[1], ALU.mult)
                link(tt(s[3], a[1], b[0], ALU.mult))
                tt(o[0], s[0], s[1], ALU.subtract)
                link(tt(o[1], s[2], s[3], ALU.add))

            s4 = [T(9 + i) for i in range(4)]
            z1 = (v(0, 1), v(1, 1))
            zp = [(z8[:, 2 * i, :], z8[:, 2 * i + 1, :]) for i in range(3)]
            z2, z4 = (T(13), T(14)), (T(0), T(1))
            z64a, z128, z256 = (T(2), T(3)), (T(4), T(5)), (T(6), T(7))
            cmul(L, z2, z1, z1, s4)
            cmul(L, z4, z2, z2, s4)
            cmul(L, zp[0], z4, z4, s4)
            cmul(L, zp[1], zp[0], zp[0], s4)
            cmul(L, zp[2], zp[1], zp[1], s4)
            cmul(L, z64a, zp[2], zp[2], s4)
            L(ts_(z64a[1], z64a[1], -1.0, None, ALU.mult))
            cmul(L, z128, z64a, z64a, s4)
            cmul(L, z256, z128, z128, s4)
            tvp = [tv[:, 256 * i:256 * i + 256] for i in range(4)]
            for arr, base in ((z64, (z64a, z128, z256)), (v4, (None, z2, z4))):
                for k, z in enumerate(base):
                    n = 1 << k
                    if z is None:
                        continue
                    if n == 1:
                        tt(arr[:, 0, :, 1], z[0], z[0], ALU.max)
                        L(tt(arr[:, 1, :, 1], z[1], z[1], ALU.max))
                        continue
                    for half in range(n * P // 256 if n * P > 256 else 1):
                        cols = slice(half * (256 // n), (half + 1) * (256 // n))
                        w = 256 // n
                        bc = [zi[:, cols].unsqueeze(2).broadcast_to([P, w, n]) for zi in z]
                        cmul(L, [arr[:, i, cols, n:2 * n] for i in range(2)],
                             [arr[:, i, cols, 0:n] for i in range(2)], bc,
                             [x.rearrange("p (g b) -> p g b", b=n) for x in tvp])
                if arr is z64:
                    dve.sem_inc(z_ready, 1)

            def v_gen(g):
                fs = Steps(dve, fv_step, 6)
                fs.start(g)
                for i in range(2):
                    last = dve.tensor_copy(vz[:, i, :, 0:8], v4[:, i, bass.ds(g * J, J), :])
                fs.link(last)
                for k in range(3):
                    n = 8 << k
                    z = [z8[:, 2 * k + i, bass.ds(g * J, J)].unsqueeze(2).broadcast_to([P, J, n]) for i in range(2)]
                    s = [x.rearrange("p (j b) -> p j b", b=n) for x in (tv[:, 256 * i:256 * i + J * n] for i in range(4))]
                    a = [vz[:, i, :, 0:n] for i in range(2)]
                    tt(s[0], a[0], z[0], ALU.mult)
                    tt(s[1], a[1], z[1], ALU.mult)
                    tt(s[2], a[0], z[1], ALU.mult)
                    fs.link(tt(s[3], a[1], z[0], ALU.mult))
                    tt(vz[:, 0, :, n:2 * n], s[0], s[1], ALU.subtract)
                    last = tt(vz[:, 1, :, n:2 * n], s[2], s[3], ALU.add)
                    if k < 2:
                        fs.link(last)
                fs.end()
                last.then_inc(v_ready, 1)

            ln_steps = [sem("ln1_step"), sem("ln2_step")]

            def layernorm(g, which, src, dst, ready):
                ls = Steps(dve, ln_steps[which], 14, waited_dve)
                ls.start(g)
                ls.link(dve.bn_stats(bn[:, which, :], src), alone=True)
                ls.link(dve.bn_aggr(mv[:, which, :], bn[:, which, :]))
                v, y, w = var[:, which, 0:1], rs[:, which:which + 1], var[:, which, 1:2]
                ls.link(ts_(v, mv[:, which, 1:2], EPS, None, ALU.add))
                ls.link(ts_(w.bitcast(I32), v.bitcast(I32), 1, None, ALU.arith_shift_right))
                ls.link(ts_(y.bitcast(I32), w.bitcast(I32), -1.0, float(0x5F3759DF), ALU.mult, ALU.add))
                for _ in range(3):
                    ls.link(stt(w, y, v, y, ALU.mult, ALU.mult))
                    ls.link(ts_(w, w, -0.5, 1.5, ALU.mult, ALU.add))
                    ls.link(tt(y, y, w, ALU.mult))
                ls.end()
                ts_(dst, src, mv[:, which, 0:1], rs[:, which:which + 1], ALU.subtract, ALU.mult).then_inc(ready, 1)

            hnew_step = sem("h_new_step")

            def front_ln(g):
                dve.wait_ge(htok_done, g + 1)
                dve.tensor_copy(h_new[:, :], bank[6][:, :]).then_inc(hnew_step, 1)
                dve.wait_ge(hnew_step, g + 1)
                layernorm(g, 0, h_new[:, :], xn[:, :], xn_ready)

            def dt_in(g):
                ms = Steps(dve, mv_step, 2)
                ms.start(g)
                dve.tensor_copy(h_cur[:, :], h_new[:, :])
                dve.wait_ge(dtraw_done, g + 1)
                sc = tv[:, 0:P].rearrange("p (k j) -> p k j", j=J)
                ms.link(tt(sc, bank[0][:, 0:P].rearrange("p (k j) -> p k j", j=J),
                           diag[:, :].unsqueeze(1).broadcast_to([P, NCK, J]), ALU.mult))
                ms.link(dve.tensor_reduce(dr[:, 0, :], sc, AX.X, ALU.add))
                stt(dr[:, 1, :], dr[:, 0, :], -1.0, dr[:, 0, :], ALU.mult, ALU.min).then_inc(dtin_ready, 1)
                ms.end()

            def dt_out(g):
                dve.wait_ge(sp_ready, g + 1)
                stt(dr[:, 3, :], dr[:, 0, :], 0.0, dr[:, 2, :], ALU.max, ALU.add).then_inc(dt_ready, 1)

            def silu(g):
                for b in range(2):
                    dve.wait_ge(sigmoid_ready, 2 * g + b + 1)
                    part = gt[:, 4 * b:4 * b + 4, :]
                    tt(part, part, bank[1 + b][:, :].rearrange("p (q t) -> p q t", q=4), ALU.mult).then_inc(g_ready, 1)

            def chunks(g):
                for k in range(4):
                    dve.wait_ge(bxtr_done, 4 * g + k + 1)
                    if k == 0:
                        dve.wait_ge(decay_ready, g + 1)
                    src = bank[1 + k % 2][:, :].rearrange("p (c hh x) -> p c hh x", c=2, hh=2)
                    dve.tensor_copy(xp[:, 4 * k:4 * k + 4, :], bank[1 + k % 2][:, :].rearrange("p (c x) -> p c x", c=4)[:, :, DS:P])
                    dec = dcy[:, 4 * k:4 * k + 4].rearrange("p (c hh) -> p c hh", hh=2)[:, :, 0]
                    tt(bd[:, 2 * k:2 * k + 2, :], src[:, :, 0, 0:DS],
                       dec.unsqueeze(2).broadcast_to([P, 2, DS]), ALU.mult).then_inc(xp_ready, 1)
                for k in range(4):
                    dve.wait_ge(scores_done, 4 * g + k + 1)
                    dve.wait_ge(em_ready, 4 * g + k + 1)
                    part = rd[:, 4 * k:4 * k + 4, :]
                    tt(part, part, bank[4 + k % 2][:, :].rearrange("p (c i) -> p c i", c=4), ALU.mult).then_inc(p_ready, 1)
                dve.wait_ge(e0_ready, 2 * g + 2)
                tt(ct_ck[:, :, 1, :], ct_ck[:, :, 1, :], e0[:, :, :], ALU.mult).then_inc(cts_ready, 1)

            def gate_y(g):
                for b in range(2):
                    dve.wait_ge(y_done, 2 * g + b + 1)
                    part = gt[:, :, 64 * b:64 * b + 64]
                    tt(part, part, bank[1 + b][:, :].rearrange("p (t q) -> p q t", q=8), ALU.mult).then_inc(yg_ready, 1)

            h2_step = sem("h2_step")

            def main_out(g, tail):
                dve.wait_ge(out_done, g + 1)
                if tail:
                    dve.wait_ge(s_h3, 16 * g)
                tt(h2[:, :], h_cur[:, :], bank[7][:, :], ALU.add).then_inc(h2_step, 1)
                dve.wait_ge(h2_step, g + 1)
                if tail:
                    dve.wait_ge(s_scat, 16 * TOPK * g)
                layernorm(g, 1, h2[:, :], xn2[:, :], xn2_ready)

            NS = 21

            def route(g):
                rs_ = Steps(dve, tv_step, NS, waited_dve)
                rs_.start(g)
                K = rs_.link
                s = s_rt[:, 2, :]
                dve.wait_ge(logits_done, g + 1)
                tt(s_rt[:, 0, :], bank[0][:, 0:EXP], brow[:, :], ALU.add).then_inc(lsum_ready, 1)
                dve.wait_ge(rexp2_ready, g + 1)
                K(ts_(s_rt[:, 1, :], s_rt[:, 1, :], 1.0, None, ALU.add))
                K(dve.reciprocal(s, s_rt[:, 1, :]))
                sm = s.rearrange("p (g pr m) -> p g pr m", pr=2, m=2)
                hi = gp[:, 0:2, :].rearrange("p a b -> p (a b)").rearrange("p (g pr) -> p g pr", pr=2)
                lo = gp[:, 2:4, :].rearrange("p a b -> p (a b)").rearrange("p (g pr) -> p g pr", pr=2)
                tt(hi, sm[:, :, :, 0], sm[:, :, :, 1], ALU.max)
                K(tt(lo, sm[:, :, :, 0], sm[:, :, :, 1], ALU.min))
                tt(gp[:, 4, :], hi[:, :, 0], hi[:, :, 1], ALU.max)
                tt(gp[:, 5, :], hi[:, :, 0], hi[:, :, 1], ALU.min)
                K(tt(gp[:, 6, :], lo[:, :, 0], lo[:, :, 1], ALU.max))
                K(tt(gp[:, 5, :], gp[:, 5, :], gp[:, 6, :], ALU.max))
                K(tt(gp[:, 7, :], gp[:, 4, :], gp[:, 5, :], ALU.add), alone=True)
                K(dve.max(top[:, :], gp[:, 7, :]), alone=True)
                K(dve.max_index(gix[:, :], top[:, :], gp[:, 7, :]))
                K(dve.tensor_copy(tixf[:, 0, :], gix[:, :]))
                eq = oh[:, 0, 0, :].rearrange("p (k g) -> p k g", k=GTOP)
                K(tt(eq, iota[:, 0:GROUPS].unsqueeze(1).broadcast_to([P, GTOP, GROUPS]),
                     tixf[:, 0, 0:GTOP].unsqueeze(2).broadcast_to([P, GTOP, GROUPS]), ALU.is_equal))
                K(dve.tensor_reduce(gp[:, 8, :], eq.rearrange("p k g -> p g k"), AX.X, ALU.add))
                mk = s_rt[:, 0, :]
                K(tt(mk.rearrange("p (g m) -> p g m", m=GSZ), s.rearrange("p (g m) -> p g m", m=GSZ),
                     gp[:, 8, :].unsqueeze(2).broadcast_to([P, GROUPS, GSZ]), ALU.mult), alone=True)
                K(dve.max(top[:, :], mk), alone=True)
                K(dve.max_index(tix[:, :], top[:, :], mk))
                K(dve.tensor_copy(tixf[:, 1, :], tix[:, :]))
                K(tt(oh[:, 0, :, :], iota[:, :].unsqueeze(1).broadcast_to([P, TOPK, EXP]),
                     tixf[:, 1, 0:TOPK].unsqueeze(2).broadcast_to([P, TOPK, EXP]), ALU.is_equal))
                dve.tensor_reduce(msk[:, :], oh[:, 0, :, :].rearrange("p k e -> p e k"), AX.X, ALU.add).then_inc(mask_ready, 1)
                K(tt(oh[:, 1, :, :], oh[:, 0, :, :], s.unsqueeze(1).broadcast_to([P, TOPK, EXP]), ALU.mult))
                K(dve.tensor_reduce(posf[:, 0:TOPK], oh[:, 1, :, :], AX.X, ALU.add))
                K(dve.tensor_reduce(gsum[:, 0:1], posf[:, 0:TOPK], AX.X, ALU.add))
                K(ts_(gsum[:, 1:2], gsum[:, 0:1], 1e-20, None, ALU.add))
                K(dve.reciprocal(gsum[:, 1:2], gsum[:, 1:2]))
                ts_(gate[:, bass.ds(g, 1), 0:TOPK].rearrange("p a k -> p (a k)"), posf[:, 0:TOPK], gsum[:, 1:2], SCALE, ALU.mult, ALU.mult)
                rs_.end()

            rank_step = sem("rank_step")

            def place(g):
                rs_ = Steps(dve, rank_step, 3)
                rs_.start(g)
                dve.wait_ge(rank_done, g + 1)
                rs_.link(tt(oh[:, 1, :, :], oh[:, 0, :, :],
                            bank[7][:, 0:EXP].unsqueeze(1).broadcast_to([P, TOPK, EXP]), ALU.mult))
                rs_.link(dve.tensor_reduce(posf[:, 0:TOPK], oh[:, 1, :, :], AX.X, ALU.add))
                rs_.link(stt(slot_now[:, :], tixf[:, 1, 0:TOPK], float(CAP), posf[:, 0:TOPK], ALU.mult, ALU.add))
                rs_.end()
                dve.tensor_copy(chosen[:, bass.ds(g, 1), 0:TOPK].rearrange("p a k -> p (a k)"), tixf[:, 1, 0:TOPK])
                dve.tensor_copy(place_in[:, bass.ds(g, 1), 0:TOPK].rearrange("p a k -> p (a k)"), posf[:, 0:TOPK])
                tt(macc[:, :], macc[:, :], msk[:, :], ALU.add).then_inc(slot_ready, 1)

            def shared(g):
                dve.wait_ge(down_done, g + 1)
                tt(h2[:, :], h2[:, :], bank[3][:, :], ALU.add).then_inc(h3_ready, 1)

            dve.memset(x2T[:, :, :], 0.0).then_inc(zeros_ready, 1)
            dve.wait_ge(k_const, 1)
            dve.wait_ge(s_ws, 16 * 5)
            v_gen(0)
            front_ln(0)

            def iteration(g, first=False, last=False):
                dt_in(g)
                if not last:
                    v_gen(g + 1)
                dt_out(g)
                silu(g)
                if not first:
                    route(g - 1)
                chunks(g)
                if not first:
                    shared(g - 1)
                if not last:
                    front_ln(g + 1)
                if not first:
                    place(g - 1)
                gate_y(g)
                main_out(g, not first)

            iteration(0, first=True)
            with dve.Fori(1, NT - 1) as g:
                iteration(g)
            iteration(NT - 1, last=True)
            route(NT - 1)
            place(NT - 1)
            shared(NT - 1)

            tb = Steps(dve, tb_step)
            B = tb.link
            dve.wait_ge(counts_done, 1)
            cnt, ntile = tv[0:EXP, 0:P], tv[0:EXP, P:P + EXP]
            ni = tv[0:EXP, P + EXP:P + 2 * EXP].bitcast(I32)
            B(dve.tensor_copy(cnt, bank[7][0:EXP, 0:P]))
            B(ts_(ni, cnt[:, 0:EXP], float(P - 1), None, ALU.add))
            B(ts_(ni, ni, 7, None, ALU.arith_shift_right))
            ts_(ntile, ni, 1.0, None, ALU.max).then_inc(tiles_ready, 1)
            dve.wait_ge(table_done, 1)
            B(dve.tensor_copy(behind[:, :], bank[6][:, 0:EXP]))
            B(dve.tensor_copy(table[:, 0:2 * EXP], bank[5][0:1, 0:2 * EXP]))
            last_start, first = tv[0:1, 192:192 + EXP], tv[0:1, 224:224 + NT]
            list_base = tv[0:1, 256:256 + EXP]
            rows, starts = tv[0:1, 512:1024].rearrange("p (e i) -> p e i", e=EXP), tp[0:1, 0, :].rearrange("p (e i) -> p e i", e=EXP)
            B(ts_(last_start, bank[5][0:1, 2 * EXP:3 * EXP], -float(P), 0.0, ALU.add, ALU.max))
            B(ts_(first, iota[0:1, 0:NT], float(P), None, ALU.mult))
            B(ts_(list_base, iota[0:1, :], float(CAP), None, ALU.mult))
            B(tt(starts, first.unsqueeze(1).broadcast_to([1, EXP, NT]), last_start.unsqueeze(2).broadcast_to([1, EXP, NT]), ALU.min))
            for k, base in enumerate((list_base, behind[0:1, :])):
                B(tt(rows, starts, base.unsqueeze(2).broadcast_to([1, EXP, NT]), ALU.add))
                B(dve.tensor_copy(table[:, (2 + NT * k) * EXP:(2 + NT * k + NT) * EXP], tv[0:1, 512:1024]))
            tt(tv[0:1, 0:1], tv[0:1, 0:1], tv[0:1, 0:1], ALU.max).then_inc(table_ready, 1)
            dve.wait_ge(table_ready, 1)

            def copy_x(tile):
                dve.wait_ge(x_in, 16 * (tile + 2))
                dve.wait_ge(trx_done, tile)
                dve.tensor_copy(xs, x_ring[:, slot_of(tile)]).then_inc(xs_ready, 1)

            dve.wait_ge(x_in, 32)
            dve.wait_ge(x2T_done, NT)
            dve.tensor_copy(xs, x_ring[:, 0:D]).then_inc(xs_ready, 1)
            with dve.Fori(0, EXP) as e:
                base, n = expert_of(dve, e)
                with dve.Fori(0, n) as i:
                    tile = dve.snap(base + i)
                    copy_x(tile + 1)
                    dve.wait_ge(y_free, tile + 1)
                    dve.wait_ge(y2_done, tile + 1)
                    dve.tensor_copy(y_ring[:, slot_of(tile)], bank[3][:, :]).then_inc(y_ready, 1)

            def picks(g, par):
                ps = Steps(dve, pick_step, 3)
                ps.start(g)
                now = lambda kept: kept[:, bass.ds(g, 1), 0:TOPK].rearrange("p a k -> p (a k)")
                ps.link(tt(oh[:, 0, :, :], iota[:, :].unsqueeze(1).broadcast_to([P, TOPK, EXP]),
                           now(chosen).unsqueeze(2).broadcast_to([P, TOPK, EXP]), ALU.is_equal))
                ps.link(tt(oh[:, 1, :, :], oh[:, 0, :, :], behind[:, :].unsqueeze(1).broadcast_to([P, TOPK, EXP]), ALU.mult))
                ps.link(dve.tensor_reduce(posf[:, 0:TOPK], oh[:, 1, :, :], AX.X, ALU.add))
                ps.end()
                tt(pick[:, par, :], posf[:, 0:TOPK], now(place_in), ALU.add).then_inc(pick_ready, 1)
                dve.tensor_copy(gnow[:, par, :], gate[:, bass.ds(g, 1), 0:TOPK].rearrange("p a k -> p (a k)")).then_inc(gate_ready, 1)

            def combine(pair, par, last=False):
                g = 2 * pair + par
                cs = Steps(dve, comb_step, TOPK - 1)
                cs.start(g)
                dve.wait_ge(gate_ready, g + 1)
                dve.wait_ge(got_h3[par], 16 * (pair + 1))
                dve.wait_ge(got[par], 16 * TOPK * (pair + 1))
                wait_out(pair, par)
                o = comb[par][:, 7 * D:8 * D]
                for k in range(TOPK):
                    ins = stt(o, comb[par][:, D * k:D * k + D], gnow[:, par, k:k + 1],
                              comb[par][:, 6 * D:7 * D] if k == 0 else o, ALU.mult, ALU.add)
                    if k < TOPK - 1:
                        cs.link(ins)
                cs.end()
                ins.then_inc(o_ready, 1)
                if not last:
                    dve.wait_ge(o_ready, g + 1)
                    picks(g + 2, par)

            def wait_out(pair, par):
                if isinstance(pair, int) and pair == 0:
                    return
                dve.wait_ge(o_out[par], 16 * NB * pair)

            for par in range(2):
                picks(par, par)
            for par in range(2):
                combine(0, par)
            with dve.Fori(1, NT // 2 - 1) as pair:
                for par in range(2):
                    combine(pair, par)
            for par in range(2):
                combine(NT // 2 - 1, par, last=True)

        @block.tensor
        def _(pe):
            def hgen(g):
                pe.wait_ge(v_ready, g + 1)
                pe.wait_ge(w_ready, g + 1)
                for j in range(J):
                    for par in range(2):
                        for i in range(2):
                            mm = pe.matmul(bank[6][64 * par:64 * par + 64, 64 * j:64 * j + 64], vz[:, i, j, :],
                                           wd[:, i, j, :, par, :], start=(i == 0), stop=(i == 1))
                mm.then_inc(hgen_done, 1)

            def four_transposes(dst, src, done):
                for k in range(KT):
                    mm = pe.transpose(dst[:, P * k:P * k + P], src(k), ident[:, :])
                mm.then_inc(done, 1)

            def tr_h(g):
                pe.wait_ge(hT_ready, g + 1)
                four_transposes(bank[6], lambda k: xT[:, k, :], htok_done)

            def tr_x(g):
                pe.wait_ge(xn_ready, g + 1)
                four_transposes(bank[6], lambda k: xn[:, P * k:P * k + P], xnT_done)

            def project(dst, w, cols, n, done):
                for m in range(n):
                    for k in range(KT):
                        mm = pe.matmul(dst[:, P * m:P * m + P], w[:, k, cols + P * m:cols + P * m + P], xT[:, k, :],
                                       start=(k == 0), stop=(k == KT - 1))
                mm.then_inc(done, 1)

            def projections(g, tail):
                pe.wait_ge(xnT_ready, g + 1)
                if not (isinstance(g, int) and g == 0):
                    pe.wait_ge(st_ready, g)
                project(bank[0], w_dt, 0, 1, dtraw_done)
                for k in range(4):
                    if k < 2:
                        if not (isinstance(g, int) and g == 0):
                            pe.wait_ge(yg_ready, 2 * g - 1 + k)
                    else:
                        pe.wait_ge(bx_copied, 4 * g + k - 1)
                    project(bank[1 + k % 2], w_bx, 512 * k, 4, bx_done)
                for b in range(2):
                    pe.wait_ge(bx_copied, 4 * g + 3 + b)
                    project(bank[1 + b], w_c, 512 * b, 4, c_done)
                if tail:
                    tr_x2(g - 1)
                for b in range(2):
                    pe.wait_ge(c_copied, 2 * g + 1 + b)
                    project(bank[1 + b], w_r, 512 * b, 4, res_done)

            def tr_x2(g):
                pe.wait_ge(xn2_ready, g + 1)
                if not (isinstance(g, int) and g == 0):
                    pe.wait_ge(h3_ready, g)
                four_transposes(bank[3], lambda k: xn2[:, P * k:P * k + P], x2T_done)

            def experts_in(g, dtin):
                pe.wait_ge(x2T_ready, g + 1)
                if dtin is not None:
                    pe.wait_ge(dtin_ready, dtin)
                for k in range(KT):
                    mm = pe.matmul(bank[0][:, 0:EXP], x2T[:, k, :], w_rt[:, k, :], start=(k == 0), stop=(k == KT - 1))
                mm.then_inc(logits_done, 1)
                for m in range(KT):
                    for k in range(KT):
                        mm = pe.matmul(bank[3][:, P * m:P * m + P], w_s1[:, k, P * m:P * m + P], x2T[:, k, :],
                                       start=(k == 0), stop=(k == KT - 1))
                mm.then_inc(up_done, 1)

            def decays(g, tail):
                pe.wait_ge(dt_ready, g + 1)
                if tail:
                    pe.wait_ge(lsum_ready, g)
                pe.matmul(bank[0][:, 0:NCK], m_gt[:, :], dr[:, 3, :], start=True, stop=True).then_inc(sigma_done, 1)
                pe.wait_ge(rd_ready, g + 1)
                for b in range(2):
                    if not (isinstance(g, int) and g == 0):
                        pe.wait_ge(p_ready, 4 * g - 1 + b)
                    pe.matmul(bank[4 + b][0:DS, :], ones[:, 0:DS], rd_half[:, 4 * b:4 * b + 4, 1, :],
                              start=True, stop=True).then_inc(e0_done, 1)
                for k in range(4):
                    if k < 2:
                        pe.wait_ge(e0_ready, 2 * g + 1 + k)
                    else:
                        pe.wait_ge(e_ready, 4 * g + k - 1)
                    pe.matmul(bank[4 + k % 2][:, :], m_gt[:, :], rd[:, 4 * k:4 * k + 4, :], start=True, stop=True).then_inc(d_done, 1)

            def scores(g):
                for k in range(4):
                    if k < 2:
                        pe.wait_ge(g_ready, 2 * g + 1 + k)
                    else:
                        pe.wait_ge(xp_ready, 4 * g + k - 1)
                    for i in range(4):
                        mm = pe.transpose(bank[1 + k % 2][:, P * i:P * i + P], bx_ck[:, 4 * k + i, :], ident[:, :])
                    mm.then_inc(bxtr_done, 1)
                for k in range(4):
                    if k < 2:
                        pe.wait_ge(e_ready, 4 * g + 3 + k)
                    else:
                        pe.wait_ge(p_ready, 4 * g + k - 1)
                    for i in range(4):
                        ck = 4 * k + i
                        mm = pe.matmul(bank[4 + k % 2][:, P * i:P * i + P], bx_ck[0:DS, ck, :], ct_ck[:, ck // 2, ck % 2, :],
                                       start=True, stop=True)
                    mm.then_inc(scores_done, 1)

            def experts_out(g):
                pe.wait_ge(us_ready, g + 1)
                for k in range(KT):
                    mm = pe.matmul(bank[3][:, :], us[:, k, :], w_s2[:, k, :], start=(k == 0), stop=(k == KT - 1))
                mm.then_inc(down_done, 1)

            def states(g):
                pe.wait_ge(xp_ready, 4 * g + 4)
                pe.wait_ge(decay_ready, g + 1)
                for c in range(NB):
                    mm = pe.matmul(bank[0][0:DS, DH * c:DH * c + DH], bd[:, c, :], xp[:, 2 * c, :], start=True, stop=True)
                mm.then_inc(st_done, 1)

            def outputs(g):
                pe.wait_ge(st_ready, g + 1)
                pe.wait_ge(cts_ready, g + 1)
                rd_par = rd[:, :, :].rearrange("p k (j q par) -> p k par j q", q=8, par=2)
                ct_par = ct[:, :].rearrange("p (k j q par) -> p k par j q", j=J, q=8, par=2)
                for b in range(2):
                    pe.wait_ge(p_ready, 4 * g + 2 * b + 2)
                    for n in range(8):
                        ck = 8 * b + n
                        for par in range(2):
                            dst = bank[1 + b][64 * par:64 * par + 64, 64 * n:64 * n + 64]
                            mm = pe.matmul(dst, xp[:, ck, :], rd_par[:, ck, par], start=True, stop=(ck % 2 == 0))
                            if ck % 2:
                                mm = pe.matmul(dst, st[:, ck // 2, :], ct_par[:, ck, par], start=False, stop=True)
                    mm.then_inc(y_done, 1)

            def ranks(g):
                pe.wait_ge(mask_ready, g + 1)
                pe.matmul(bank[7][:, 0:EXP], m_lt[:, :], msk[:, :], start=True, stop=False)
                pe.matmul(bank[7][:, 0:EXP], ones[:, :], macc[:, :], start=False, stop=True).then_inc(rank_done, 1)

            def project_out(g, tail):
                pe.wait_ge(yg_ready, 2 * g + 2)
                if tail:
                    pe.wait_ge(slot_ready, g)
                for k in range(8):
                    mm = pe.matmul(bank[7][:, :], gt[:, k, :], w_o[:, k, :], start=(k == 0), stop=(k == 7))
                mm.then_inc(out_done, 1)

            pe.wait_ge(k_const, 1)
            hgen(0)
            tr_h(0)
            tr_x(0)
            pe.wait_ge(s_wf, 16 * 4)
            pe.wait_ge(s_ws, 16 * 5)

            def iteration(g, first=False, last=False):
                projections(g, not first)
                if not first:
                    experts_in(g - 1, g + 1)
                decays(g, not first)
                if not last:
                    hgen(g + 1)
                scores(g)
                if not first:
                    experts_out(g - 1)
                if not last:
                    tr_h(g + 1)
                states(g)
                if not first:
                    ranks(g - 1)
                outputs(g)
                if not last:
                    tr_x(g + 1)
                project_out(g, not first)

            iteration(0, first=True)
            with pe.Fori(1, NT - 1) as g:
                iteration(g)
            iteration(NT - 1, last=True)
            tr_x2(NT - 1)
            pe.wait_ge(st_ready, NT)
            experts_in(NT - 1, None)
            ranks(NT - 1)
            experts_out(NT - 1)

            pe.wait_ge(slot_ready, NT)
            pe.matmul(bank[7][0:EXP, 0:P], macc[:, :], ones[:, :], start=True, stop=True).then_inc(counts_done, 1)
            pe.wait_ge(tiles_ready, 1)
            cnt, ntile = tv[0:EXP, 0:P], tv[0:EXP, P:P + EXP]
            pe.matmul(bank[6][:, 0:EXP], cnt, m_lt[0:EXP, 0:EXP], start=True, stop=True)
            for k, (a, b) in enumerate(((ntile, m_lt), (ntile, ident), (cnt[:, 0:EXP], ident))):
                mm = pe.matmul(bank[5][0:EXP, EXP * k:EXP * k + EXP], a, b[0:EXP, 0:EXP], start=True, stop=True)
            mm.then_inc(table_done, 1)

            def turn_x(tile):
                pe.wait_ge(xs_ready, tile + 1 + RING)
                four_transposes(bank[2], lambda k: xs[:, P * k:P * k + P], trx_done)

            pe.wait_ge(table_ready, 1)
            pe.sem_inc(y_ready, 1)
            turn_x(0)
            pe.wait_ge(w_first, 16 * WB)

            def expert(four, par):
                base, n = expert_of(pe, WB * four + par)
                if not isinstance(four, int):
                    wait_alone(pe, w_in[par], 16 * four, waited_pe)
                with pe.Fori(0, n) as i:
                    tile = pe.snap(base + i)
                    pe.wait_ge(xsT_ready, tile + 1)
                    for m in range(2):
                        for k in range(KT):
                            mm = pe.matmul(bank[m][:, 0:P], w1[par][:, k, P * m:P * m + P], xsT[:, k, :],
                                           start=(k == 0), stop=(k == KT - 1))
                        mm.then_inc(h_done, 1)
                    turn_x(tile + 1)
                    pe.wait_ge(y_ready, tile + 1)
                    for m in range(2):
                        pe.wait_ge(hu_ready, 2 * tile + m + 1)
                        mm = pe.matmul(bank[3][:, :], hu[:, m, :], w2[par][:, m, :], start=(m == 0), stop=(m == 1))
                    mm.then_inc(y2_done, 1)

            for par in range(WB):
                expert(0, par)
            with pe.Fori(1, EXP // WB) as four:
                for par in range(WB):
                    expert(four, par)


def tile_of(tiles, g):
    if isinstance(g, int):
        return tiles[g]
    return tiles[bass.ds(g, 1)].rearrange("o a b c -> (o a) b c" if len(tiles.shape) == 4 else "o a b -> (o a) b")


_LAYOUTS = ("s4d", "c_tiles", "w_dt", "w_bx", "w_c", "w_r", "w_o", "w_rt", "w_s1", "w_s2", "br", "experts")


def layouts(x, log_dt, B_ri, inv_A_real, A_imag, w_in, w_param, w_out, Wr, br, W1, W2, Ws1, Ws2):
    def rows(a):
        return a.reshape(NT, 2, J, DS).transpose(1, 3, 0, 2).reshape(P, P)

    def contract(w):
        o, i = w.shape
        return np.ascontiguousarray(w.T.reshape(i // P, P, o).transpose(1, 0, 2))

    s4d = np.stack([rows(inv_A_real), rows(A_imag), rows(np.broadcast_to(log_dt[:, None], (NH, DS))),
                    rows(B_ri[..., 0]), rows(B_ri[..., 1])], axis=1)
    c = x.reshape(NB, NT, 2, J, DS, 2).transpose(1, 2, 4, 5, 3, 0).reshape(NT, P, 2, J * NB)
    wp = w_param.reshape(HEADS, 1 + 2 * DS, D)
    wi = w_in.reshape(2, HEADS, DH, D)
    w_bx = np.concatenate([wp[:, 1:1 + DS], wi[0]], axis=1).reshape(HEADS * P, D)
    d = {
        "s4d": s4d, "c_tiles": c, "w_bx": contract(w_bx), "w_c": contract(wp[:, 1 + DS:].reshape(HEADS * DS, D)),
        "w_r": contract(wi[1].reshape(HEADS * DH, D)),
        "w_dt": contract(np.broadcast_to(wp[None, :, 0], (J, HEADS, D)).reshape(P, D)),
        "w_o": contract(w_out), "w_rt": contract(Wr), "w_s1": contract(Ws1), "w_s2": contract(Ws2),
        "br": np.broadcast_to(br[None, :], (P, EXP)),
        "experts": np.stack([np.concatenate([contract(W1[e]).reshape(P, -1), contract(W2[e]).reshape(P, -1)], axis=1)
                             for e in range(EXP)]),
    }
    return {k: np.ascontiguousarray(v) for k, v in d.items()}


def kernel(x, L0_tok_log_dt, L0_tok_B_ri, L0_tok_inv_A_real, L0_tok_A_imag, L0_attn_w_in, L0_attn_w_param,
           L0_attn_w_out, L0_ffn_Wr, L0_ffn_br, L0_ffn_W1, L0_ffn_W2, L0_ffn_Ws1, L0_ffn_Ws2):
    import concourse.bacc as bacc
    from concourse.bass_utils import run_bass_kernel_spmd

    arrays = layouts(*(np.asarray(a) for a in (
        x, L0_tok_log_dt, L0_tok_B_ri, L0_tok_inv_A_real, L0_tok_A_imag, L0_attn_w_in, L0_attn_w_param,
        L0_attn_w_out, L0_ffn_Wr, L0_ffn_br, L0_ffn_W1, L0_ffn_W2, L0_ffn_Ws1, L0_ffn_Ws2)))
    nc = bacc.Bacc("TRN2", target_bir_lowering=False, num_devices=1)
    t = {k: nc.dram_tensor(f"in_{k}", a.shape, F32, kind="ExternalInput").ap() for k, a in arrays.items()}
    t["out"] = nc.dram_tensor("out_0", (NB, NH, D), F32, kind="ExternalOutput").ap()
    build(nc, t)
    r = run_bass_kernel_spmd(nc, [{f"in_{k}": a for k, a in arrays.items()}], core_ids=[0])
    return r.results[0]["out_0"]
```

```python
import numpy as np
import concourse.bass as bass
from concourse import mybir
from contextlib import ExitStack

F32 = mybir.dt.float32
I32 = mybir.dt.int32
U32 = mybir.dt.uint32
ALU = mybir.AluOpType
ACT = mybir.ActivationFunctionType
AX = mybir.AxisListType

P = 128
NB, NH, D = 8, 256, 512
NT = NB * NH // P
J = 8
HEADS, DS, DH = 16, 64, 64
NCK = 16
KT = D // P
EXP, MH, TOPK, GROUPS, GTOP = 32, 256, 6, 8, 4
GSZ = EXP // GROUPS
SCALE = 2.5
EPS = 1e-5
CAP = NT * P + P


def wait_alone(engine, sem, value, counted):
    engine.wait_ge(sem, value)
    if not isinstance(value, int):
        engine.sem_inc(counted, 1)


class Steps:

    def __init__(self, engine, sem, per_tile=0, counted=None):
        self.engine, self.sem, self.per_tile, self.counted = engine, sem, per_tile, counted
        self.base, self.n = 0, 0

    def start(self, tile):
        self.base, self.n = tile * self.per_tile, 0

    def link(self, instruction, alone=False):
        self.n += 1
        instruction.then_inc(self.sem, 1)
        if alone:
            wait_alone(self.engine, self.sem, self.base + self.n, self.counted)
        else:
            self.engine.wait_ge(self.sem, self.base + self.n)

    def end(self):
        assert self.n == self.per_tile, (self.n, self.per_tile)


def build(nc, t):
    ctx = ExitStack()
    with ctx:

        def sb(name, shape, dt=F32):
            return ctx.enter_context(nc.sbuf_tensor(name, shape, dt))

        def sem(name):
            return ctx.enter_context(nc.semaphore(name))

        w_bx = sb("w_bx", [P, KT, HEADS * P])
        w_c = sb("w_c", [P, KT, HEADS * DS])
        w_r = sb("w_r", [P, KT, HEADS * DH])
        w_dt = sb("w_dt", [P, KT, P])
        w_o = sb("w_o", [P, 8, D])
        w_s1 = sb("w_s1", [P, KT, D])
        w_s2 = sb("w_s2", [P, KT, D])
        w_rt = sb("w_rt", [P, KT, EXP])
        brow = sb("brow", [P, EXP])
        ident = sb("ident", [P, P])
        m_gt = sb("m_gt", [P, P])
        m_le = sb("m_le", [P, P])
        m_lt = sb("m_lt", [P, P])
        ones = sb("ones", [P, P])
        diag = sb("diag", [P, J])
        iota = sb("iota", [P, EXP])
        z8 = sb("z8", [P, 6, P])
        v4 = sb("v4", [P, 2, P, 8])
        z64 = sb("z64", [P, 2, P, 8])
        q = sb("q", [P, 2, P])
        c_in = sb("c_in", [P, 2, J * NB])
        vz = sb("vz", [P, 2, J, 64])
        wd = sb("wd", [P, 2, J, 2, 2, 32])
        w0 = sb("w0", [P, 2, J, NB])
        tp = sb("tp", [P, 2, J * 64])
        tv = sb("tv", [P, 1024])
        xT = sb("xT", [P, KT, P])
        h_new = sb("h_new", [P, D])
        h_cur = sb("h_cur", [P, D])
        h2 = sb("h2", [P, D])
        xn = sb("xn", [P, D])
        xn2 = sb("xn2", [P, D])
        x2T = sb("x2T", [P, KT, P])
        bx = sb("bx", [P, P * HEADS])
        ct = sb("ct", [DS, P * HEADS])
        gt = sb("gt", [P, 8, P])
        rd = sb("rd", [P, NCK, P])
        e0 = sb("e0", [DS, NB, P])
        xp = sb("xp", [P, NCK, DH])
        bd = sb("bd", [P, NB, DS])
        st = sb("st", [DS, NB, DH])
        us = sb("us", [P, KT, P])
        dr = sb("dr", [P, 4, NCK])
        dcy = sb("dcy", [P, NCK])
        bn = sb("bn", [P, 2, 6])
        mv = sb("mv", [P, 2, 2])
        rs = sb("rs", [P, 2])
        var = sb("var", [P, 2, 2])
        s_rt = sb("s_rt", [P, 3, EXP])
        oh = sb("oh", [P, 2, TOPK, EXP])
        gp = sb("gp", [P, 9, GROUPS])
        gsum = sb("gsum", [P, 4])
        gix = sb("gix", [P, 8], U32)
        top = sb("top", [P, 8])
        tix = sb("tix", [P, 8], U32)
        tixf = sb("tixf", [P, 2, 8])
        msk = sb("msk", [P, EXP])
        macc = sb("macc", [P, EXP])
        posf = sb("posf", [P, 8])
        table = sb("table", [1, 2, P + EXP], I32)
        experts = sb("experts", [1, 2, EXP], I32)
        first_rows = sb("first_rows", [P, 2])
        number = sb("number", [P, 1])
        behind = sb("behind", [P, EXP])
        pick = sb("pick", [P, 4, TOPK], U32)
        gnow = sb("gnow", [P, 4, TOPK])
        slot_now = sb("slot_now", [P, TOPK], U32)
        chosen = sb("chosen", [P, NT, 8])
        place_in = sb("place_in", [P, NT, 8])
        gate = sb("gate", [P, NT, 8])

        bank = [ctx.enter_context(nc.psum_tensor(f"bank{i}", [P, 512], F32)) for i in range(8)]

        lists = nc.dram_tensor("expert_rows", [EXP * CAP, D], F32, kind="Internal").ap()
        results = nc.dram_tensor("expert_results", [NT * P * TOPK + P, D], F32, kind="Internal").ap()
        h3_dram = nc.dram_tensor("h_and_shared", [NT, P, D], F32, kind="Internal").ap()

        s_pre = sem("s4d_inputs_loaded")
        loaded = {n: sem(f"{n}_loaded") for n in ("w_dt", "w_bx", "w_c", "w_r", "w_o", "w_rt", "w_s1", "w_s2", "br")}
        s_cin = sem("c_loaded")
        s_h3 = sem("h3_stored")
        s_scat = sem("rows_scattered")
        k_const = sem("constants_ready")
        pool_step = sem("pool_prologue_step")
        dve_pre = sem("dve_prologue_step")
        s_exps = sem("prologue_exps")
        z_ready = sem("z_powers_ready")
        fv_step, fp_step = sem("front_dve_step"), sem("front_pool_step")
        v_ready, w_ready = sem("v_ready"), sem("w_ready")
        hgen_done, hT_ready, htok_done = sem("hgen_done"), sem("hT_ready"), sem("htok_done")
        xn_ready, xnT_done, xnT_ready = sem("xn_ready"), sem("xnT_done"), sem("xnT_ready")
        h2_step = sem("h2_step")
        mv_step, ma_step = sem("main_dve_step"), sem("main_act_step")
        dtraw_done, dtin_ready, sp_ready, dt_ready = (sem(n) for n in ("dtraw_done", "dtin_ready", "sp_ready", "dt_ready"))
        bx_done, bx_copied, c_done, c_copied = (sem(n) for n in ("bx_done", "bx_copied", "c_done", "c_copied"))
        res_done, sigmoid_ready, silu_step, g_ready = (sem(n) for n in ("res_done", "sigmoid_ready", "silu_step", "g_ready"))
        sigma_done, decay_ready, rd_ready = (sem(n) for n in ("sigma_done", "decay_ready", "rd_ready"))
        e0_done, e0_ready, d_done, e_ready, em_ready = (sem(n) for n in ("e0_done", "e0_ready", "d_done", "e_ready", "em_ready"))
        bxtr_done, xp_ready, scores_done, p_ready, cts_ready = (sem(n) for n in ("bxtr_done", "xp_ready", "scores_done", "p_ready", "cts_ready"))
        st_done, st_ready, y_done, yg_ready, out_done, xn2_ready = (sem(n) for n in ("st_done", "st_ready", "y_done", "yg_ready", "out_done", "xn2_ready"))
        tv_step, ta_step = sem("tail_dve_step"), sem("tail_act_step")
        x2T_done, x2T_ready, logits_done, rexp2_ready, lsum_ready = (sem(n) for n in ("x2T_done", "x2T_ready", "logits_done", "router_exp_ready", "logits_ready"))
        up_done, us_ready, down_done, h3_ready = (sem(n) for n in ("up_done", "us_ready", "down_done", "h3_ready"))
        mask_ready, rank_done, slot_ready = (sem(n) for n in ("mask_ready", "rank_done", "slot_ready"))

        out_tiles = [t["out"][c] for c in range(NB)]
        block = ctx.enter_context(nc.Block())

        waited_dve, waited_pool, waited_sp, waited_pe = (sem(f"waited_{e}") for e in ("dve", "pool", "sp", "pe"))
        pre = bx[:, 0:5 * P].rearrange("p (k x) -> p k x", k=5)
        tmp = rd[:, :, :].rearrange("p (a b) i -> p a (b i)", a=16)

        ct_hd = ct[:, :].rearrange("p (t q par) -> p t q par", q=8, par=2)
        ct_ck = ct[:, :].rearrange("p (c hh i) -> p c hh i", c=NB, hh=2)
        bx_hd = bx[:, :].rearrange("p (t h) -> p t h", h=HEADS)
        bx_ck = bx[:, :].rearrange("p (k i) -> p k i", i=P)
        rd_half = rd[:, :, :].rearrange("p (c hh) i -> p c hh i", hh=2)

        WB = 4
        w_exp = [w_bx[:, 0, :], w_bx[:, 1, :]]
        w_exp += [w_o[:, 4 * i:4 * i + 4, :].rearrange("p k d -> p (k d)") for i in range(2)]
        w1 = [w_exp[par][:, 0:KT * MH].rearrange("p (k m) -> p k m", k=KT) for par in range(WB)]
        w2 = [w_exp[par][:, KT * MH:].rearrange("p (k d) -> p k d", k=MH // P) for par in range(WB)]
        x_ring, y_ring = w_bx[:, 2, :], w_bx[:, 3, :]
        xs, xsT, hu = xn[:, :], xT, us[:, 0:2, :]
        CB = 4
        comb = [w[:, :, :].rearrange("p k n -> p (k n)") for w in (w_c, w_r, w_bx[:, 0:2, :], w_bx[:, 2:4, :])]
        zeros_ready, zeros_in = sem("zeros_ready"), sem("zeros_stored")
        counts_done, tiles_ready, sums_done, first_rows_ready, turned, table_ready = (sem(n) for n in (
            "counts_done", "tiles_ready", "sums_done", "first_rows_ready", "rows_turned", "table_ready"))
        tb_step, rings_done = sem("table_step"), sem("rings_done")
        w_first, w_in = sem("first_experts_loaded"), [sem(f"expert_weights_loaded{i}") for i in range(4)]
        x_in, xs_ready, trx_done, xsT_ready = (sem(n) for n in ("x_tile_loaded", "xs_ready", "xs_transposed", "xsT_ready"))
        h_done, relu_step, hu_ready = (sem(n) for n in ("h_done", "relu_step", "hu_ready"))
        y2_done, y_ready, y_out, y_free = (sem(n) for n in ("expert_y_done", "expert_y_ready", "expert_y_stored", "y_slots_freed"))
        gate_ready, pick_step = sem("gates_ready"), sem("pick_step")
        pick_ready, got_h3 = sem("picks_ready"), [sem(f"h3_loaded{i}") for i in range(CB)]
        got = [sem(f"results_gathered{i}") for i in range(CB)]
        comb_step, o_ready = sem("combine_step"), sem("out_tile_ready")
        o_out = [sem(f"out_tile_stored{i}") for i in range(CB)]
        RING = 4

        def expert_of(engine, e):
            return (engine.value_load(experts[0:1, 0, bass.ds(e, 1)], min_val=0, max_val=NT * TOPK + EXP),
                    engine.value_load(experts[0:1, 1, bass.ds(e, 1)], min_val=1, max_val=NT))

        def all_tiles(engine):
            before, own = expert_of(engine, EXP - 1)
            return engine.snap(before + own)

        def list_row(engine, tile):
            return engine.value_load(table[0:1, 0, bass.ds(tile, 1)], min_val=0, max_val=EXP * CAP - P)

        def result_row(engine, tile):
            return engine.value_load(table[0:1, 1, bass.ds(tile, 1)], min_val=0, max_val=NT * P * TOPK)

        def slot_of(tile):
            return bass.ds((tile % RING) * D, D)

        @block.sync
        def _(sp):
            sp.dma_start(pre, t["s4d"]).then_inc(s_pre, 16)
            sp.dma_start(c_in[:, :, :], t["c_tiles"][0]).then_inc(s_cin, 16)
            for dst, name in ((w_dt, "w_dt"), (w_bx, "w_bx"), (w_c, "w_c"), (w_r, "w_r"), (w_o, "w_o"),
                              (w_rt, "w_rt"), (w_s1, "w_s1"), (w_s2, "w_s2")):
                sp.dma_start(dst[:, :, :], t[name]).then_inc(loaded[name], 16)
            sp.dma_start(brow[:, :], t["br"]).then_inc(loaded["br"], 16)

            def load_c(g):
                wait_alone(sp, w_ready, g, waited_sp)
                sp.dma_start(c_in[:, :, :], tile_of(t["c_tiles"], g)).then_inc(s_cin, 16)

            def store_h3(g):
                wait_alone(sp, h3_ready, g + 1, waited_sp)
                sp.dma_start(tile_of(h3_dram, g), h2[:, :]).then_inc(s_h3, 16)

            sp.wait_ge(zeros_ready, 1)
            with sp.Fori(0, EXP) as e:
                sp.dma_start(lists.rearrange("(e r) d -> e r d", e=EXP)[bass.ds(e, 1), 0:P, :].rearrange("o r d -> (o r) d"),
                             x2T[:, :, :].rearrange("p k t -> p (k t)")).then_inc(zeros_in, 16)
            load_c(1)
            load_c(2)
            with sp.Fori(1, NT - 2) as g:
                load_c(g + 2)
                store_h3(g - 1)
            store_h3(NT - 3)
            store_h3(NT - 2)
            sp.wait_ge(res_done, 2 * NT)
            for par in range(WB):
                if par == 2:
                    sp.wait_ge(out_done, NT)
                sp.dma_start(w_exp[par], t["experts"][par]).then_inc(w_first, 16)
            store_h3(NT - 1)

            sp.wait_ge(table_ready, 1)
            sp.wait_ge(s_scat, 16 * TOPK * NT)
            sp.sem_inc(xs_ready, RING)
            sp.sem_inc(y_free, RING - 1)
            sp.sem_inc(x_in, 16)
            sp.sem_inc(y_out, 16)

            def load_x(tile):
                row = list_row(sp, tile)
                wait_alone(sp, xs_ready, tile + 1, waited_sp)
                wait_alone(sp, x_in, 16 * (tile + 1), waited_sp)
                sp.dma_start(x_ring[:, slot_of(tile)], lists[bass.ds(row, P), :]).then_inc(x_in, 16)

            def store_y(tile):
                row = result_row(sp, tile)
                wait_alone(sp, y_ready, tile + 2, waited_sp)
                wait_alone(sp, y_out, 16 * (tile + 1), waited_sp)
                sp.dma_start(results[bass.ds(row, P), :], y_ring[:, slot_of(tile)]).then_inc(y_out, 16)
                sp.sem_inc(y_free, 1)

            tiles = all_tiles(sp)
            with sp.Fori(0, RING) as tile:
                load_x(tile)
            with sp.Fori(0, tiles) as tile:
                store_y(tile)
                load_x(tile + RING)
            wait_alone(sp, y_out, 16 * (tiles + 1), waited_sp)
            wait_alone(sp, x_in, 16 * (tiles + RING + 1), waited_sp)
            sp.sem_inc(rings_done, 1)

            sp.wait_ge(s_h3, 16 * NT)

            def load_h3(g, par):
                sp.dma_start(comb[par][:, 6 * D:7 * D], tile_of(h3_dram, g)).then_inc(got_h3[par], 16)

            def store_out(four, par):
                wait_alone(sp, o_ready, CB * four + par + 1, waited_sp)
                for c in range(NB):
                    sp.dma_start(out_tiles[c][bass.ds((CB * four + par) * 16, 16), :],
                                 comb[par][16 * c:16 * c + 16, 7 * D:8 * D]).then_inc(o_out[par], 16)

            for par in range(CB):
                load_h3(par, par)
            with sp.Fori(0, NT // CB - 1) as four:
                for par in range(CB):
                    store_out(four, par)
                    load_h3(CB * four + CB + par, par)
            for par in range(CB):
                store_out(NT // CB - 1, par)
            for par in range(CB):
                sp.wait_ge(o_out[par], 16 * NB * NT // CB)

        @block.gpsimd
        def _(pool):
            step = Steps(pool, pool_step)
            for m in (ident, m_gt, m_le, m_lt, ones):
                pool.memset(m[:, :], 0.0 if m is ident else 1.0)
            pool.memset(diag[:, :], 1.0)
            pool.iota(number[:, :], pattern=[[1, 1]], base=0, channel_multiplier=1,
                      allow_small_or_imprecise_dtypes=True)
            pool.memset(macc[:, :], 0.0)
            pool.iota(iota[:, :], pattern=[[1, EXP]], base=0, channel_multiplier=0,
                      allow_small_or_imprecise_dtypes=True)
            step.link(pool.memset(wd[:, :, :, :, :, :], 0.0))
            pool.affine_select(out=ident[:, :], in_=ident[:, :], compare_op=ALU.not_equal, fill=1.0,
                               base=0, pattern=[[-1, P]], channel_multiplier=1)
            pool.affine_select(out=m_gt[:, :], in_=m_gt[:, :], compare_op=ALU.is_gt, fill=0.0,
                               base=0, pattern=[[-1, P]], channel_multiplier=1)
            pool.affine_select(out=m_le[:, :], in_=m_le[:, :], compare_op=ALU.is_ge, fill=0.0,
                               base=0, pattern=[[1, P]], channel_multiplier=-1)
            pool.affine_select(out=m_lt[:, :], in_=m_lt[:, :], compare_op=ALU.is_gt, fill=0.0,
                               base=0, pattern=[[1, P]], channel_multiplier=-1)
            step.link(pool.affine_select(out=diag[:, :], in_=diag[:, :], compare_op=ALU.is_ge, fill=0.0,
                                         base=0, pattern=[[-HEADS, J]], channel_multiplier=1))
            pool.affine_select(out=diag[:, :], in_=diag[:, :], compare_op=ALU.is_gt, fill=0.0,
                               base=HEADS, pattern=[[HEADS, J]], channel_multiplier=-1).then_inc(k_const, 1)

            def front(g):
                fs = Steps(pool, fp_step, 7, waited_pool)
                fs.start(g)
                pool.wait_ge(s_cin, (g + 1) * 16)
                if not (isinstance(g, int) and g == 0):
                    wait_alone(pool, hgen_done, g, waited_pool)
                C = lambda i: c_in[:, i, :].rearrange("p (j c) -> p j c", j=J)
                Q = lambda i: q[:, i, bass.ds(g * J, J)].unsqueeze(2).broadcast_to([P, J, NB])
                T8 = lambda i: tp[:, i, 0:J * NB].rearrange("p (j c) -> p j c", j=J)
                pool.tensor_tensor(T8(0), C(0), Q(0), ALU.mult)
                fs.link(pool.tensor_tensor(T8(1), C(1), Q(1), ALU.mult))
                fs.link(pool.tensor_tensor(w0[:, 0, :, :], T8(0), T8(1), ALU.add), alone=True)
                pool.tensor_tensor(T8(0), C(0), Q(1), ALU.mult)
                fs.link(pool.tensor_tensor(T8(1), C(1), Q(0), ALU.mult))
                fs.link(pool.tensor_tensor(w0[:, 1, :, :], T8(0), T8(1), ALU.subtract), alone=True)
                W = lambda i: w0[:, i, :, :].unsqueeze(3).broadcast_to([P, J, NB, 8])
                Z = lambda i: z64[:, i, bass.ds(g * J, J), :].unsqueeze(2).broadcast_to([P, J, NB, 8])
                T = lambda i: tp[:, i, :].rearrange("p (j c a) -> p j c a", j=J, c=NB)
                for i, (za, zb, op) in enumerate(((0, 1, ALU.subtract), (1, 0, ALU.add))):
                    pool.tensor_tensor(T(0), W(0), Z(za), ALU.mult)
                    fs.link(pool.tensor_tensor(T(1), W(1), Z(zb), ALU.mult))
                    for hh in range(2):
                        lanes = slice(64 * hh, 64 * hh + 64)
                        V = lambda k: tp[lanes, k, :].rearrange("p (j m par) -> p j par m", j=J, par=2)
                        last = pool.tensor_tensor(wd[lanes, i, :, hh, :, :], V(0), V(1), op)
                    if i == 0:
                        fs.link(last, alone=True)
                fs.end()
                last.then_inc(w_ready, 1)
                pool.wait_ge(w_ready, g + 1)

            def dt_tri(g):
                pool.wait_ge(dt_ready, g + 1)
                if not (isinstance(g, int) and g == 0):
                    pool.wait_ge(y_done, 2 * g)
                pool.tensor_tensor(rd[:, :, :], m_le[:, :].unsqueeze(1).broadcast_to([P, NCK, P]),
                                   dr[:, 3, :].unsqueeze(2).broadcast_to([P, NCK, P]), ALU.mult).then_inc(rd_ready, 1)

            def causal(g):
                for k in range(4):
                    wait_alone(pool, e_ready, 4 * g + k + 1, waited_pool)
                    part = rd[:, 4 * k:4 * k + 4, :]
                    pool.affine_select(out=part, in_=part, compare_op=ALU.is_ge, fill=0.0, base=0,
                                       pattern=[[0, 4], [1, P]], channel_multiplier=-1).then_inc(em_ready, 1)

            def scatter(g):
                wait_alone(pool, slot_ready, g + 1, waited_pool)
                for k in range(TOPK):
                    pool.indirect_dma_start(
                        out=lists, out_offset=bass.IndirectOffsetOnAxis(ap=slot_now[:, k:k + 1], axis=0),
                        in_=xn2[:, :], in_offset=None).then_inc(s_scat, 16)
                pool.wait_ge(s_scat, 16 * TOPK * (g + 1))

            pool.wait_ge(z_ready, 1)
            front(0)

            def iteration(g, first=False, last=False):
                if not last:
                    front(g + 1)
                dt_tri(g)
                causal(g)
                if not first:
                    scatter(g - 1)

            pool.wait_ge(z_ready, 2)
            iteration(0, first=True)
            pool.wait_ge(zeros_in, 16 * EXP)
            with pool.Fori(1, NT - 1) as g:
                iteration(g)
            iteration(NT - 1, last=True)
            scatter(NT - 1)

            pool.wait_ge(table_ready, 1)
            with pool.Fori(0, EXP // WB - 1) as four:
                for par in range(WB):
                    e = WB * four + par
                    base, n = expert_of(pool, e)
                    wait_alone(pool, y_ready, base + n + 1, waited_pool)
                    pool.dma_start(w_exp[par], t["experts"][bass.ds(e + WB, 1)].rearrange("o p n -> (o p) n")).then_inc(w_in[par], 16)

            pool.wait_ge(rings_done, 1)

            def gather(four, par):
                wait_alone(pool, pick_ready, CB * four + par + 1, waited_pool)
                for k in range(TOPK):
                    pool.indirect_dma_start(out=comb[par][:, D * k:D * k + D], out_offset=None, in_=results[0:NT * P * TOPK, :],
                                            in_offset=bass.IndirectOffsetOnAxis(ap=pick[:, par, k:k + 1], axis=0)).then_inc(got[par], 16)

            with pool.Fori(0, NT // CB) as four:
                for par in range(CB):
                    gather(four, par)

        @block.scalar
        def _(act):
            nc.scalar.preload_act_table_set("natural_log_exp_and_others")
            act.wait_ge(s_pre, 16)
            act.activation(tmp[:, 0, :], pre[:, 0, :], ACT.Exp)
            act.activation(tmp[:, 1, :], pre[:, 2, :], ACT.Exp).then_inc(s_exps, 1)

            def front_h(g):
                act.wait_ge(hgen_done, g + 1)
                src = bank[6][:, :].rearrange("p (j hh c a) -> p j hh c a", j=J, hh=2, c=NB)
                for hh in range(2):
                    for a in range(KT):
                        last = act.activation(xT[:, a, :].rearrange("p (c hh j) -> p hh c j", hh=2, j=J)[:, hh],
                                              src[:, :, hh, :, a].rearrange("p j c -> p c j"), ACT.Copy)
                last.then_inc(hT_ready, 1)

            def front_x(g):
                act.wait_ge(xnT_done, g + 1)
                act.activation(xT[:, :, :], bank[6][:, :].rearrange("p (k t) -> p k t", k=KT), ACT.Copy).then_inc(xnT_ready, 1)

            def copy_bx(g, k):
                act.wait_ge(bx_done, 4 * g + k + 1)
                act.activation(bx_hd[:, :, 4 * k:4 * k + 4], bank[1 + k % 2][:, :].rearrange("p (h t) -> p t h", h=4),
                               ACT.Copy).then_inc(bx_copied, 1)

            def main(g, tail):
                ms = Steps(act, ma_step, 1)
                ms.start(g)
                copy_bx(g, 0)
                act.wait_ge(dtin_ready, g + 1)
                ms.link(act.activation(dr[:, 2, :], dr[:, 1, :], ACT.Exp))
                act.activation(dr[:, 2, :], dr[:, 2, :], ACT.Ln, bias=1.0).then_inc(sp_ready, 1)
                ms.end()
                for k in range(1, 4):
                    copy_bx(g, k)
                for b in range(2):
                    act.wait_ge(c_done, 2 * g + b + 1)
                    for par in range(2):
                        last = act.activation(ct_hd[:, :, 4 * b:4 * b + 4, par],
                                              bank[1 + b][64 * par:64 * par + 64, :].rearrange("p (q t) -> p t q", q=4), ACT.Copy)
                    last.then_inc(c_copied, 1)
                if tail:
                    act.wait_ge(x2T_done, g)
                    act.activation(x2T[:, :, :], bank[3][:, :].rearrange("p (k t) -> p k t", k=KT), ACT.Copy).then_inc(x2T_ready, 1)
                ss = Steps(act, silu_step, 4)
                ss.start(g)
                for b in range(2):
                    act.wait_ge(res_done, 2 * g + b + 1)
                    part = gt[:, 4 * b:4 * b + 4, :]
                    ss.link(act.activation(part, bank[1 + b][:, :].rearrange("p (q t) -> p q t", q=4), ACT.Exp, scale=-1.0))
                    ss.link(act.activation(part, part, ACT.Ln, bias=1.0))
                    act.activation(part, part, ACT.Exp, scale=-1.0).then_inc(sigmoid_ready, 1)
                ss.end()
                if tail:
                    tail_a(g - 1)
                act.wait_ge(sigma_done, g + 1)
                act.activation(dcy[:, :], bank[0][:, 0:NCK], ACT.Exp, scale=-1.0).then_inc(decay_ready, 1)
                act.wait_ge(e0_done, g + 1)
                for b in range(2):
                    last = act.activation(e0[:, 4 * b:4 * b + 4, :], bank[7][DS * b:DS * b + DS, :].rearrange("p (c i) -> p c i", c=4),
                                          ACT.Exp, scale=-1.0)
                last.then_inc(e0_ready, 1)
                for k in range(4):
                    act.wait_ge(d_done, 4 * g + k + 1)
                    act.activation(rd[:, 4 * k:4 * k + 4, :], bank[4 + k % 2][:, :].rearrange("p (c i) -> p c i", c=4),
                                   ACT.Exp, scale=-1.0).then_inc(e_ready, 1)

            def tail_a(g):
                act.wait_ge(lsum_ready, g + 1)
                act.activation(s_rt[:, 1, :], s_rt[:, 0, :], ACT.Exp, scale=-1.0).then_inc(rexp2_ready, 1)
                act.wait_ge(up_done, g + 1)
                ts = Steps(act, ta_step, 1)
                ts.start(g)
                ts.link(act.activation(us[:, :, :], bank[3][:, :].rearrange("p (k t) -> p k t", k=KT), ACT.Relu))
                ts.end()
                act.activation(us[:, :, :], us[:, :, :], ACT.Square).then_inc(us_ready, 1)

            def copy_st(g):
                act.wait_ge(st_done, g + 1)
                for half in range(2):
                    last = act.activation(st[:, :, :].rearrange("p (n half) h -> p half n h", half=2)[:, half],
                                          bank[0][DS * half:DS * half + DS, 0:DH * NB // 2].rearrange("p (n h) -> p n h", h=DH), ACT.Copy)
                last.then_inc(st_ready, 1)

            front_h(0)
            front_x(0)

            def iteration(g, first=False, last=False):
                main(g, not first)
                if not last:
                    front_h(g + 1)
                copy_st(g)
                if not last:
                    front_x(g + 1)

            iteration(0, first=True)
            act.wait_ge(zeros_in, 16 * EXP)
            with act.Fori(1, NT - 1) as g:
                iteration(g)
            iteration(NT - 1, last=True)
            act.wait_ge(x2T_done, NT)
            act.activation(x2T[:, :, :], bank[3][:, :].rearrange("p (k t) -> p k t", k=KT), ACT.Copy).then_inc(x2T_ready, 1)
            tail_a(NT - 1)

            def copy_x(tile):
                act.wait_ge(trx_done, tile + 1)
                act.activation(xsT[:, :, :], bank[2][:, :].rearrange("p (k t) -> p k t", k=KT), ACT.Copy).then_inc(xsT_ready, 1)

            act.wait_ge(table_ready, 1)
            copy_x(0)
            with act.Fori(0, all_tiles(act)) as tile:
                for m in range(2):
                    act.wait_ge(h_done, 2 * tile + m + 1)
                    act.activation(hu[:, m, :], bank[m][:, 0:P], ACT.Relu).then_inc(relu_step, 1)
                    act.wait_ge(relu_step, 2 * tile + m + 1)
                    act.activation(hu[:, m, :], hu[:, m, :], ACT.Square).then_inc(hu_ready, 1)
                copy_x(tile + 1)

        @block.vector
        def _(dve):
            step = Steps(dve, dve_pre)
            L = step.link
            tt, ts_, stt = dve.tensor_tensor, dve.tensor_scalar, dve.scalar_tensor_tensor
            dve.wait_ge(s_pre, 16)
            dve.wait_ge(s_exps, 1)
            T = lambda i: tmp[:, i, :]
            nega, dt, ur, ui, t2, t3, n_, om, den = (T(i) for i in range(9))
            A_im, Br, Bi = pre[:, 1, :], pre[:, 3, :], pre[:, 4, :]
            L(stt(ur, nega, -0.5, dt, ALU.mult, ALU.mult))
            L(stt(ui, A_im, 0.5, dt, ALU.mult, ALU.mult))
            L(tt(t2, ui, ui, ALU.mult))
            L(tt(t3, ur, ur, ALU.mult))
            L(ts_(om, ur, -1.0, 1.0, ALU.mult, ALU.add))
            L(tt(n_, t2, t3, ALU.add))
            L(tt(den, om, om, ALU.mult))
            L(tt(den, den, t2, ALU.add))
            L(dve.reciprocal(den, den))
            L(ts_(n_, n_, -1.0, 1.0, ALU.mult, ALU.add))
            v = lambda i, b: v4[:, i, :, b]
            dve.memset(v4[:, 0, :, 0], 1.0)
            dve.memset(v4[:, 1, :, 0], 0.0)
            dve.memset(z64[:, 0, :, 0], 1.0)
            dve.memset(z64[:, 1, :, 0], 0.0)
            L(tt(v(0, 1), n_, den, ALU.mult))
            L(stt(v(1, 1), ui, 2.0, den, ALU.mult, ALU.mult))
            L(stt(t3, dt, 2.0, den, ALU.mult, ALU.mult))
            L(tt(t2, Br, om, ALU.mult))
            L(tt(n_, Bi, ui, ALU.mult))
            L(tt(t2, t2, n_, ALU.subtract))
            L(tt(q[:, 0, :], t2, t3, ALU.mult))
            L(tt(t2, Br, ui, ALU.mult))
            L(tt(n_, Bi, om, ALU.mult))
            L(tt(t2, t2, n_, ALU.add))
            L(stt(q[:, 1, :], t2, -1.0, t3, ALU.mult, ALU.mult))

            def cmul(link, o, a, b, s, minus=False):
                tt(s[0], a[0], b[0], ALU.mult)
                tt(s[1], a[1], b[1], ALU.mult)
                tt(s[2], a[0], b[1], ALU.mult)
                link(tt(s[3], a[1], b[0], ALU.mult))
                tt(o[0], s[0], s[1], ALU.subtract)
                link(tt(o[1], s[2], s[3], ALU.add))

            s4 = [T(9 + i) for i in range(4)]
            z1 = (v(0, 1), v(1, 1))
            zp = [(z8[:, 2 * i, :], z8[:, 2 * i + 1, :]) for i in range(3)]
            z2, z4 = (T(13), T(14)), (T(0), T(1))
            z64a, z128, z256 = (T(2), T(3)), (T(4), T(5)), (T(6), T(7))
            cmul(L, z2, z1, z1, s4)
            cmul(L, z4, z2, z2, s4)
            cmul(L, zp[0], z4, z4, s4)
            cmul(L, zp[1], zp[0], zp[0], s4)
            cmul(L, zp[2], zp[1], zp[1], s4)
            cmul(L, z64a, zp[2], zp[2], s4)
            L(ts_(z64a[1], z64a[1], -1.0, None, ALU.mult))
            cmul(L, z128, z64a, z64a, s4)
            cmul(L, z256, z128, z128, s4)
            scratch = [tv[:, 256 * i:256 * i + 256] for i in range(4)]

            def powers(first, end):
                for arr, base in ((z64, (z64a, z128, z256)), (v4, (None, z2, z4))):
                    for k, z in enumerate(base):
                        n = 1 << k
                        if z is None:
                            continue
                        if n == 1:
                            tt(arr[:, 0, first:end, 1], z[0][:, first:end], z[0][:, first:end], ALU.max)
                            L(tt(arr[:, 1, first:end, 1], z[1][:, first:end], z[1][:, first:end], ALU.max))
                            continue
                        for c in range(first, end, 256 // n):
                            cols = slice(c, min(end, c + 256 // n))
                            w = cols.stop - cols.start
                            bc = [zi[:, cols].unsqueeze(2).broadcast_to([P, w, n]) for zi in z]
                            cmul(L, [arr[:, i, cols, n:2 * n] for i in range(2)],
                                 [arr[:, i, cols, 0:n] for i in range(2)], bc,
                                 [x[:, 0:w * n].rearrange("p (g b) -> p g b", b=n) for x in scratch])
                    if arr is z64:
                        dve.sem_inc(z_ready, 1)

            powers(0, J)

            def v_gen(g):
                fs = Steps(dve, fv_step, 6)
                fs.start(g)
                for i in range(2):
                    last = dve.tensor_copy(vz[:, i, :, 0:8], v4[:, i, bass.ds(g * J, J), :])
                fs.link(last)
                for k in range(3):
                    n = 8 << k
                    z = [z8[:, 2 * k + i, bass.ds(g * J, J)].unsqueeze(2).broadcast_to([P, J, n]) for i in range(2)]
                    s = [x.rearrange("p (j b) -> p j b", b=n) for x in (tv[:, 256 * i:256 * i + J * n] for i in range(4))]
                    a = [vz[:, i, :, 0:n] for i in range(2)]
                    tt(s[0], a[0], z[0], ALU.mult)
                    tt(s[1], a[1], z[1], ALU.mult)
                    tt(s[2], a[0], z[1], ALU.mult)
                    fs.link(tt(s[3], a[1], z[0], ALU.mult))
                    tt(vz[:, 0, :, n:2 * n], s[0], s[1], ALU.subtract)
                    last = tt(vz[:, 1, :, n:2 * n], s[2], s[3], ALU.add)
                    if k < 2:
                        fs.link(last)
                fs.end()
                last.then_inc(v_ready, 1)

            ln_steps = [sem("ln1_step"), sem("ln2_step")]

            def layernorm(g, which, src, dst, ready):
                ls = Steps(dve, ln_steps[which], 14, waited_dve)
                ls.start(g)
                ls.link(dve.bn_stats(bn[:, which, :], src), alone=True)
                ls.link(dve.bn_aggr(mv[:, which, :], bn[:, which, :]))
                v, y, w = var[:, which, 0:1], rs[:, which:which + 1], var[:, which, 1:2]
                ls.link(ts_(v, mv[:, which, 1:2], EPS, None, ALU.add))
                ls.link(ts_(w.bitcast(I32), v.bitcast(I32), 1, None, ALU.arith_shift_right))
                ls.link(ts_(y.bitcast(I32), w.bitcast(I32), -1.0, float(0x5F3759DF), ALU.mult, ALU.add))
                for _ in range(3):
                    ls.link(stt(w, y, v, y, ALU.mult, ALU.mult))
                    ls.link(ts_(w, w, -0.5, 1.5, ALU.mult, ALU.add))
                    ls.link(tt(y, y, w, ALU.mult))
                ls.end()
                ts_(dst, src, mv[:, which, 0:1], rs[:, which:which + 1], ALU.subtract, ALU.mult).then_inc(ready, 1)

            hnew_step = sem("h_new_step")

            def front_ln(g):
                dve.wait_ge(htok_done, g + 1)
                dve.tensor_copy(h_new[:, :], bank[6][:, :]).then_inc(hnew_step, 1)
                dve.wait_ge(hnew_step, g + 1)
                layernorm(g, 0, h_new[:, :], xn[:, :], xn_ready)

            def dt_in(g):
                ms = Steps(dve, mv_step, 2)
                ms.start(g)
                dve.tensor_copy(h_cur[:, :], h_new[:, :])
                dve.wait_ge(dtraw_done, g + 1)
                sc = tv[:, 0:P].rearrange("p (k j) -> p k j", j=J)
                ms.link(tt(sc, bank[0][:, 0:P].rearrange("p (k j) -> p k j", j=J),
                           diag[:, :].unsqueeze(1).broadcast_to([P, NCK, J]), ALU.mult))
                ms.link(dve.tensor_reduce(dr[:, 0, :], sc, AX.X, ALU.add))
                stt(dr[:, 1, :], dr[:, 0, :], -1.0, dr[:, 0, :], ALU.mult, ALU.min).then_inc(dtin_ready, 1)
                ms.end()

            def dt_out(g):
                dve.wait_ge(sp_ready, g + 1)
                stt(dr[:, 3, :], dr[:, 0, :], 0.0, dr[:, 2, :], ALU.max, ALU.add).then_inc(dt_ready, 1)

            def silu(g):
                for b in range(2):
                    dve.wait_ge(sigmoid_ready, 2 * g + b + 1)
                    part = gt[:, 4 * b:4 * b + 4, :]
                    tt(part, part, bank[1 + b][:, :].rearrange("p (q t) -> p q t", q=4), ALU.mult).then_inc(g_ready, 1)

            def chunks(g):
                dve.wait_ge(decay_ready, g + 1)

                def positions(k):
                    dve.wait_ge(bxtr_done, 4 * g + k + 1)
                    src = bank[1 + k % 2][:, :].rearrange("p (c hh x) -> p c hh x", c=2, hh=2)
                    dve.tensor_copy(xp[:, 4 * k:4 * k + 4, :], bank[1 + k % 2][:, :].rearrange("p (c x) -> p c x", c=4)[:, :, DS:P])
                    dec = dcy[:, 4 * k:4 * k + 4].rearrange("p (c hh) -> p c hh", hh=2)[:, :, 0]
                    tt(bd[:, 2 * k:2 * k + 2, :], src[:, :, 0, 0:DS],
                       dec.unsqueeze(2).broadcast_to([P, 2, DS]), ALU.mult).then_inc(xp_ready, 1)

                def decayed(k):
                    dve.wait_ge(scores_done, 4 * g + k + 1)
                    dve.wait_ge(em_ready, 4 * g + k + 1)
                    part = rd[:, 4 * k:4 * k + 4, :]
                    tt(part, part, bank[4 + k % 2][:, :].rearrange("p (c i) -> p c i", c=4), ALU.mult).then_inc(p_ready, 1)

                for half in range(2):
                    for k in range(2):
                        positions(2 * half + k)
                    for k in range(2):
                        decayed(2 * half + k)
                dve.wait_ge(e0_ready, g + 1)
                tt(ct_ck[:, :, 1, :], ct_ck[:, :, 1, :], e0[:, :, :], ALU.mult).then_inc(cts_ready, 1)

            def gate_y(g):
                for b in range(2):
                    dve.wait_ge(y_done, 2 * g + b + 1)
                    part = gt[:, :, 64 * b:64 * b + 64]
                    tt(part, part, bank[1 + b][:, :].rearrange("p (t q) -> p q t", q=8), ALU.mult).then_inc(yg_ready, 1)

            def main_out(g, tail):
                dve.wait_ge(out_done, g + 1)
                if tail:
                    dve.wait_ge(s_h3, 16 * g)
                tt(h2[:, :], h_cur[:, :], bank[7][:, :], ALU.add).then_inc(h2_step, 1)
                dve.wait_ge(h2_step, g + 1)
                if tail:
                    dve.wait_ge(s_scat, 16 * TOPK * g)
                layernorm(g, 1, h2[:, :], xn2[:, :], xn2_ready)

            NS = 21

            def route(g):
                rs_ = Steps(dve, tv_step, NS, waited_dve)
                rs_.start(g)
                K = rs_.link
                s = s_rt[:, 2, :]
                dve.wait_ge(logits_done, g + 1)
                tt(s_rt[:, 0, :], bank[0][:, 0:EXP], brow[:, :], ALU.add).then_inc(lsum_ready, 1)
                dve.wait_ge(rexp2_ready, g + 1)
                K(ts_(s_rt[:, 1, :], s_rt[:, 1, :], 1.0, None, ALU.add))
                K(dve.reciprocal(s, s_rt[:, 1, :]))
                sm = s.rearrange("p (g pr m) -> p g pr m", pr=2, m=2)
                hi = gp[:, 0:2, :].rearrange("p a b -> p (a b)").rearrange("p (g pr) -> p g pr", pr=2)
                lo = gp[:, 2:4, :].rearrange("p a b -> p (a b)").rearrange("p (g pr) -> p g pr", pr=2)
                tt(hi, sm[:, :, :, 0], sm[:, :, :, 1], ALU.max)
                K(tt(lo, sm[:, :, :, 0], sm[:, :, :, 1], ALU.min))
                tt(gp[:, 4, :], hi[:, :, 0], hi[:, :, 1], ALU.max)
                tt(gp[:, 5, :], hi[:, :, 0], hi[:, :, 1], ALU.min)
                K(tt(gp[:, 6, :], lo[:, :, 0], lo[:, :, 1], ALU.max))
                K(tt(gp[:, 5, :], gp[:, 5, :], gp[:, 6, :], ALU.max))
                K(tt(gp[:, 7, :], gp[:, 4, :], gp[:, 5, :], ALU.add), alone=True)
                K(dve.max(top[:, :], gp[:, 7, :]), alone=True)
                K(dve.max_index(gix[:, :], top[:, :], gp[:, 7, :]))
                K(dve.tensor_copy(tixf[:, 0, :], gix[:, :]))
                eq = oh[:, 0, 0, :].rearrange("p (k g) -> p k g", k=GTOP)
                K(tt(eq, iota[:, 0:GROUPS].unsqueeze(1).broadcast_to([P, GTOP, GROUPS]),
                     tixf[:, 0, 0:GTOP].unsqueeze(2).broadcast_to([P, GTOP, GROUPS]), ALU.is_equal))
                K(dve.tensor_reduce(gp[:, 8, :], eq.rearrange("p k g -> p g k"), AX.X, ALU.add))
                mk = s_rt[:, 0, :]
                K(tt(mk.rearrange("p (g m) -> p g m", m=GSZ), s.rearrange("p (g m) -> p g m", m=GSZ),
                     gp[:, 8, :].unsqueeze(2).broadcast_to([P, GROUPS, GSZ]), ALU.mult), alone=True)
                K(dve.max(top[:, :], mk), alone=True)
                K(dve.max_index(tix[:, :], top[:, :], mk))
                K(dve.tensor_copy(tixf[:, 1, :], tix[:, :]))
                K(tt(oh[:, 0, :, :], iota[:, :].unsqueeze(1).broadcast_to([P, TOPK, EXP]),
                     tixf[:, 1, 0:TOPK].unsqueeze(2).broadcast_to([P, TOPK, EXP]), ALU.is_equal))
                dve.tensor_reduce(msk[:, :], oh[:, 0, :, :].rearrange("p k e -> p e k"), AX.X, ALU.add).then_inc(mask_ready, 1)
                K(tt(oh[:, 1, :, :], oh[:, 0, :, :], s.unsqueeze(1).broadcast_to([P, TOPK, EXP]), ALU.mult))
                K(dve.tensor_reduce(posf[:, 0:TOPK], oh[:, 1, :, :], AX.X, ALU.add))
                K(dve.tensor_reduce(gsum[:, 0:1], posf[:, 0:TOPK], AX.X, ALU.add))
                K(ts_(gsum[:, 1:2], gsum[:, 0:1], 1e-20, None, ALU.add))
                K(dve.reciprocal(gsum[:, 1:2], gsum[:, 1:2]))
                ts_(gate[:, bass.ds(g, 1), 0:TOPK].rearrange("p a k -> p (a k)"), posf[:, 0:TOPK], gsum[:, 1:2], SCALE, ALU.mult, ALU.mult)
                rs_.end()

            rank_step = sem("rank_step")

            def place(g):
                rs_ = Steps(dve, rank_step, 3)
                rs_.start(g)
                dve.wait_ge(rank_done, g + 1)
                rs_.link(tt(oh[:, 1, :, :], oh[:, 0, :, :],
                            bank[7][:, 0:EXP].unsqueeze(1).broadcast_to([P, TOPK, EXP]), ALU.mult))
                rs_.link(dve.tensor_reduce(posf[:, 0:TOPK], oh[:, 1, :, :], AX.X, ALU.add))
                rs_.link(stt(slot_now[:, :], tixf[:, 1, 0:TOPK], float(CAP), posf[:, 0:TOPK], ALU.mult, ALU.add))
                rs_.end()
                dve.tensor_copy(chosen[:, bass.ds(g, 1), 0:TOPK].rearrange("p a k -> p (a k)"), tixf[:, 1, 0:TOPK])
                dve.tensor_copy(place_in[:, bass.ds(g, 1), 0:TOPK].rearrange("p a k -> p (a k)"), posf[:, 0:TOPK])
                tt(macc[:, :], macc[:, :], msk[:, :], ALU.add).then_inc(slot_ready, 1)

            def shared(g):
                dve.wait_ge(down_done, g + 1)
                tt(h2[:, :], h2[:, :], bank[3][:, :], ALU.add).then_inc(h3_ready, 1)

            dve.memset(x2T[:, :, :], 0.0).then_inc(zeros_ready, 1)
            dve.wait_ge(k_const, 1)
            v_gen(0)
            dve.wait_ge(v_ready, 1)
            powers(J, P)
            front_ln(0)

            def iteration(g, first=False, last=False):
                dt_in(g)
                if not last:
                    v_gen(g + 1)
                dt_out(g)
                silu(g)
                if not first:
                    route(g - 1)
                chunks(g)
                if not last:
                    front_ln(g + 1)
                if not first:
                    place(g - 1)
                gate_y(g)
                if not first:
                    shared(g - 1)
                main_out(g, not first)

            iteration(0, first=True)
            dve.wait_ge(loaded["br"], 16)
            with dve.Fori(1, NT - 1) as g:
                iteration(g)
            iteration(NT - 1, last=True)
            route(NT - 1)
            place(NT - 1)
            shared(NT - 1)

            tb = Steps(dve, tb_step)
            B = tb.link
            dve.wait_ge(counts_done, 1)
            cnt, ntile = tv[0:EXP, 0:P], tv[0:EXP, P:2 * P]
            ni = tv[0:EXP, 2 * P:3 * P].bitcast(I32)
            B(dve.memset(table[:, :, :], 0))
            B(dve.tensor_copy(cnt, bank[7][0:EXP, 0:P]))
            B(ts_(ni, cnt, float(P - 1), None, ALU.add))
            B(ts_(ni, ni, 7, None, ALU.arith_shift_right))
            ts_(ntile, ni, 1.0, None, ALU.max).then_inc(tiles_ready, 1)
            dve.wait_ge(sums_done, 1)
            W = lambda k: tv[:, 512 + EXP * k:512 + EXP * (k + 1)]
            before, tiles, rows, start, inside, both = W(0), W(1), W(2), W(4), W(5), tv[:, 768:768 + 2 * EXP]
            B(dve.tensor_copy(tv[:, 512:512 + 4 * EXP], bank[5][:, 0:4 * EXP]))
            dve.tensor_copy(behind[:, :], W(3))
            B(dve.tensor_copy(experts[:, :, :], tv[0:1, 512:512 + 2 * EXP].rearrange("p (a e) -> p a e", a=2)))
            B(tt(tiles, before, tiles, ALU.add))
            B(ts_(inside, before, number[:, 0:1], None, ALU.is_le))
            B(stt(inside, tiles, number[:, 0:1], inside, ALU.is_gt, ALU.mult))
            B(ts_(rows, rows, -float(P), 0.0, ALU.add, ALU.max))
            B(ts_(start, before, number[:, 0:1], -float(P), ALU.subtract, ALU.mult))
            B(tt(start, start, rows, ALU.min))
            B(stt(both[:, 0:EXP], iota[:, :], float(CAP), start, ALU.mult, ALU.add))
            B(tt(both[:, EXP:], start, W(3), ALU.add))
            pair = both.rearrange("p (a e) -> p a e", a=2)
            B(tt(pair, pair, inside.unsqueeze(1).broadcast_to([P, 2, EXP]), ALU.mult))
            dve.tensor_reduce(first_rows[:, :], pair, AX.X, ALU.add).then_inc(first_rows_ready, 1)
            dve.wait_ge(turned, 1)
            dve.tensor_copy(table[:, :, 0:P], bank[4][0:1, 0:2 * P].rearrange("p (a t) -> p a t", a=2)).then_inc(table_ready, 1)
            dve.wait_ge(table_ready, 1)

            def copy_x(tile):
                dve.wait_ge(x_in, 16 * (tile + 2))
                dve.wait_ge(trx_done, tile)
                dve.tensor_copy(xs, x_ring[:, slot_of(tile)]).then_inc(xs_ready, 1)

            dve.wait_ge(x_in, 32)
            dve.wait_ge(x2T_done, NT)
            dve.tensor_copy(xs, x_ring[:, 0:D]).then_inc(xs_ready, 1)
            with dve.Fori(0, all_tiles(dve)) as tile:
                copy_x(tile + 1)
                dve.wait_ge(y_free, tile + 1)
                dve.wait_ge(y2_done, tile + 1)
                dve.tensor_copy(y_ring[:, slot_of(tile)], bank[3][:, :]).then_inc(y_ready, 1)

            def picks(g, par):
                ps = Steps(dve, pick_step, 3)
                ps.start(g)
                now = lambda kept: kept[:, bass.ds(g, 1), 0:TOPK].rearrange("p a k -> p (a k)")
                ps.link(tt(oh[:, 0, :, :], iota[:, :].unsqueeze(1).broadcast_to([P, TOPK, EXP]),
                           now(chosen).unsqueeze(2).broadcast_to([P, TOPK, EXP]), ALU.is_equal))
                ps.link(tt(oh[:, 1, :, :], oh[:, 0, :, :], behind[:, :].unsqueeze(1).broadcast_to([P, TOPK, EXP]), ALU.mult))
                ps.link(dve.tensor_reduce(posf[:, 0:TOPK], oh[:, 1, :, :], AX.X, ALU.add))
                ps.end()
                tt(pick[:, par, :], posf[:, 0:TOPK], now(place_in), ALU.add).then_inc(pick_ready, 1)
                dve.tensor_copy(gnow[:, par, :], gate[:, bass.ds(g, 1), 0:TOPK].rearrange("p a k -> p (a k)")).then_inc(gate_ready, 1)

            def combine(four, par, last=False):
                g = CB * four + par
                cs = Steps(dve, comb_step, TOPK - 1)
                cs.start(g)
                dve.wait_ge(gate_ready, g + 1)
                dve.wait_ge(got_h3[par], 16 * (four + 1))
                dve.wait_ge(got[par], 16 * TOPK * (four + 1))
                wait_out(four, par)
                o = comb[par][:, 7 * D:8 * D]
                for k in range(TOPK):
                    ins = stt(o, comb[par][:, D * k:D * k + D], gnow[:, par, k:k + 1],
                              comb[par][:, 6 * D:7 * D] if k == 0 else o, ALU.mult, ALU.add)
                    if k < TOPK - 1:
                        cs.link(ins)
                cs.end()
                ins.then_inc(o_ready, 1)
                if not last:
                    dve.wait_ge(o_ready, g + 1)
                    picks(g + CB, par)

            def wait_out(four, par):
                if isinstance(four, int) and four == 0:
                    return
                dve.wait_ge(o_out[par], 16 * NB * four)

            for par in range(CB):
                picks(par, par)
            for par in range(CB):
                combine(0, par)
            with dve.Fori(1, NT // CB - 1) as four:
                for par in range(CB):
                    combine(four, par)
            for par in range(CB):
                combine(NT // CB - 1, par, last=True)

        @block.tensor
        def _(pe):
            def hgen(g):
                pe.wait_ge(v_ready, g + 1)
                pe.wait_ge(w_ready, g + 1)
                for j in range(J):
                    for par in range(2):
                        for i in range(2):
                            mm = pe.matmul(bank[6][64 * par:64 * par + 64, 64 * j:64 * j + 64], vz[:, i, j, :],
                                           wd[:, i, j, :, par, :], start=(i == 0), stop=(i == 1))
                mm.then_inc(hgen_done, 1)

            def four_transposes(dst, src, done):
                for k in range(KT):
                    mm = pe.transpose(dst[:, P * k:P * k + P], src(k), ident[:, :])
                mm.then_inc(done, 1)

            def tr_h(g):
                pe.wait_ge(hT_ready, g + 1)
                four_transposes(bank[6], lambda k: xT[:, k, :], htok_done)

            def tr_x(g):
                pe.wait_ge(xn_ready, g + 1)
                four_transposes(bank[6], lambda k: xn[:, P * k:P * k + P], xnT_done)

            def project(dst, w, cols, n, done):
                for m in range(n):
                    for k in range(KT):
                        mm = pe.matmul(dst[:, P * m:P * m + P], w[:, k, cols + P * m:cols + P * m + P], xT[:, k, :],
                                       start=(k == 0), stop=(k == KT - 1))
                mm.then_inc(done, 1)

            def projections(g, tail):
                pe.wait_ge(xnT_ready, g + 1)
                if not (isinstance(g, int) and g == 0):
                    pe.wait_ge(st_ready, g)
                first = isinstance(g, int) and g == 0
                if first:
                    pe.wait_ge(loaded["w_dt"], 16)
                project(bank[0], w_dt, 0, 1, dtraw_done)
                if first:
                    pe.wait_ge(loaded["w_bx"], 16)
                for k in range(4):
                    if k < 2:
                        if not (isinstance(g, int) and g == 0):
                            pe.wait_ge(yg_ready, 2 * g - 1 + k)
                    else:
                        pe.wait_ge(bx_copied, 4 * g + k - 1)
                    project(bank[1 + k % 2], w_bx, 512 * k, 4, bx_done)
                if first:
                    pe.wait_ge(loaded["w_c"], 16)
                for b in range(2):
                    pe.wait_ge(bx_copied, 4 * g + 3 + b)
                    project(bank[1 + b], w_c, 512 * b, 4, c_done)
                if tail:
                    tr_x2(g - 1)
                if first:
                    pe.wait_ge(loaded["w_r"], 16)
                for b in range(2):
                    pe.wait_ge(c_copied, 2 * g + 1 + b)
                    project(bank[1 + b], w_r, 512 * b, 4, res_done)

            def tr_x2(g):
                pe.wait_ge(xn2_ready, g + 1)
                if not (isinstance(g, int) and g == 0):
                    pe.wait_ge(h3_ready, g)
                four_transposes(bank[3], lambda k: xn2[:, P * k:P * k + P], x2T_done)

            def experts_in(g, dtin):
                pe.wait_ge(x2T_ready, g + 1)
                if dtin is not None:
                    pe.wait_ge(dtin_ready, dtin)
                for k in range(KT):
                    mm = pe.matmul(bank[0][:, 0:EXP], x2T[:, k, :], w_rt[:, k, :], start=(k == 0), stop=(k == KT - 1))
                mm.then_inc(logits_done, 1)
                for m in range(KT):
                    for k in range(KT):
                        mm = pe.matmul(bank[3][:, P * m:P * m + P], w_s1[:, k, P * m:P * m + P], x2T[:, k, :],
                                       start=(k == 0), stop=(k == KT - 1))
                mm.then_inc(up_done, 1)

            def decays(g, tail):
                pe.wait_ge(dt_ready, g + 1)
                if tail:
                    pe.wait_ge(lsum_ready, g)
                pe.matmul(bank[0][:, 0:NCK], m_gt[:, :], dr[:, 3, :], start=True, stop=True).then_inc(sigma_done, 1)
                pe.wait_ge(rd_ready, g + 1)
                later = not (isinstance(g, int) and g == 0)
                if later:
                    pe.wait_ge(h2_step, g)
                for b in range(2):
                    mm = pe.matmul(bank[7][DS * b:DS * b + DS, :], ones[:, 0:DS], rd_half[:, 4 * b:4 * b + 4, 1, :],
                                   start=True, stop=True)
                mm.then_inc(e0_done, 1)
                for k in range(4):
                    if k >= 2:
                        pe.wait_ge(e_ready, 4 * g + k - 1)
                    elif later:
                        pe.wait_ge(p_ready, 4 * g - 1 + k)
                    pe.matmul(bank[4 + k % 2][:, :], m_gt[:, :], rd[:, 4 * k:4 * k + 4, :], start=True, stop=True).then_inc(d_done, 1)

            def scores(g):
                def turn_bx(k):
                    if k < 2:
                        pe.wait_ge(g_ready, 2 * g + 1 + k)
                    else:
                        pe.wait_ge(xp_ready, 4 * g + k - 1)
                    for i in range(4):
                        mm = pe.transpose(bank[1 + k % 2][:, P * i:P * i + P], bx_ck[:, 4 * k + i, :], ident[:, :])
                    mm.then_inc(bxtr_done, 1)

                def score(k):
                    if k < 2:
                        pe.wait_ge(e_ready, 4 * g + 3 + k)
                    else:
                        pe.wait_ge(p_ready, 4 * g + k - 1)
                    for i in range(4):
                        ck = 4 * k + i
                        mm = pe.matmul(bank[4 + k % 2][:, P * i:P * i + P], bx_ck[0:DS, ck, :], ct_ck[:, ck // 2, ck % 2, :],
                                       start=True, stop=True)
                    mm.then_inc(scores_done, 1)

                for half in range(2):
                    for k in range(2):
                        turn_bx(2 * half + k)
                    for k in range(2):
                        score(2 * half + k)

            def experts_out(g):
                experts_out_part(g, 0, 1)
                experts_out_part(g, 1, KT)

            def experts_out_part(g, begin, end):
                if begin == 0:
                    pe.wait_ge(us_ready, g + 1)
                for k in range(begin, end):
                    mm = pe.matmul(bank[3][:, :], us[:, k, :], w_s2[:, k, :], start=(k == 0), stop=(k == KT - 1))
                if end == KT:
                    mm.then_inc(down_done, 1)

            def states(g):
                pe.wait_ge(xp_ready, 4 * g + 4)
                pe.wait_ge(decay_ready, g + 1)
                for c in range(NB):
                    half, n = c % 2, c // 2
                    mm = pe.matmul(bank[0][DS * half:DS * half + DS, DH * n:DH * n + DH], bd[:, c, :], xp[:, 2 * c, :],
                                   start=True, stop=True)
                mm.then_inc(st_done, 1)

            def outputs(g):
                pe.wait_ge(st_ready, g + 1)
                pe.wait_ge(cts_ready, g + 1)
                rd_par = rd[:, :, :].rearrange("p k (j q par) -> p k par j q", q=8, par=2)
                ct_par = ct[:, :].rearrange("p (k j q par) -> p k par j q", j=J, q=8, par=2)
                for b in range(2):
                    pe.wait_ge(p_ready, 4 * g + 2 * b + 2)
                    for n in range(8):
                        ck = 8 * b + n
                        for par in range(2):
                            dst = bank[1 + b][64 * par:64 * par + 64, 64 * n:64 * n + 64]
                            mm = pe.matmul(dst, xp[:, ck, :], rd_par[:, ck, par], start=True, stop=(ck % 2 == 0))
                            if ck % 2:
                                mm = pe.matmul(dst, st[:, ck // 2, :], ct_par[:, ck, par], start=False, stop=True)
                    mm.then_inc(y_done, 1)

            def ranks(g, now):
                pe.wait_ge(e0_ready, now + 1)
                pe.wait_ge(mask_ready, g + 1)
                pe.matmul(bank[7][:, 0:EXP], m_lt[:, :], msk[:, :], start=True, stop=False)
                pe.matmul(bank[7][:, 0:EXP], ones[:, :], macc[:, :], start=False, stop=True).then_inc(rank_done, 1)

            def project_out(g, tail):
                pe.wait_ge(yg_ready, 2 * g + 2)
                if tail:
                    pe.wait_ge(slot_ready, g)
                else:
                    pe.wait_ge(loaded["w_o"], 16)
                for k in range(8):
                    mm = pe.matmul(bank[7][:, :], gt[:, k, :], w_o[:, k, :], start=(k == 0), stop=(k == 7))
                mm.then_inc(out_done, 1)

            pe.wait_ge(k_const, 1)
            hgen(0)
            tr_h(0)
            tr_x(0)

            def iteration(g, first=False, last=False):
                projections(g, not first)
                if not first:
                    experts_in(g - 1, g + 1)
                decays(g, not first)
                if not last:
                    hgen(g + 1)
                scores(g)
                states(g)
                if not last:
                    tr_h(g + 1)
                if not first:
                    ranks(g - 1, g)
                    experts_out_part(g - 1, 0, 1)
                outputs(g)
                if not first:
                    experts_out_part(g - 1, 1, KT)
                if not last:
                    tr_x(g + 1)
                project_out(g, not first)

            iteration(0, first=True)
            for name in ("w_rt", "w_s1", "w_s2"):
                pe.wait_ge(loaded[name], 16)
            with pe.Fori(1, NT - 1) as g:
                iteration(g)
            iteration(NT - 1, last=True)
            tr_x2(NT - 1)
            pe.wait_ge(st_ready, NT)
            experts_in(NT - 1, None)
            ranks(NT - 1, NT - 1)
            experts_out(NT - 1)

            pe.wait_ge(slot_ready, NT)
            pe.matmul(bank[7][0:EXP, 0:P], macc[:, :], ones[:, :], start=True, stop=True).then_inc(counts_done, 1)
            pe.wait_ge(tiles_ready, 1)
            cnt, ntile = tv[0:EXP, 0:P], tv[0:EXP, P:2 * P]
            for k, (a, b) in enumerate(((ntile, m_lt), (ntile, ident), (cnt, ident), (cnt, m_lt))):
                mm = pe.matmul(bank[5][:, EXP * k:EXP * k + EXP], a, b[0:EXP, 0:EXP], start=True, stop=True)
            mm.then_inc(sums_done, 1)
            pe.wait_ge(first_rows_ready, 1)
            for k in range(2):
                mm = pe.matmul(bank[4][0:1, P * k:P * k + P], first_rows[:, k:k + 1], ident[:, :], start=True, stop=True)
            mm.then_inc(turned, 1)

            def turn_x(tile):
                pe.wait_ge(xs_ready, tile + 1 + RING)
                four_transposes(bank[2], lambda k: xs[:, P * k:P * k + P], trx_done)

            pe.wait_ge(table_ready, 1)
            pe.sem_inc(y_ready, 1)
            turn_x(0)
            pe.wait_ge(w_first, 16 * WB)

            def expert(four, par):
                base, n = expert_of(pe, WB * four + par)
                if not isinstance(four, int):
                    wait_alone(pe, w_in[par], 16 * four, waited_pe)
                with pe.Fori(0, n) as i:
                    tile = pe.snap(base + i)
                    pe.wait_ge(xsT_ready, tile + 1)
                    for m in range(2):
                        for k in range(KT):
                            mm = pe.matmul(bank[m][:, 0:P], w1[par][:, k, P * m:P * m + P], xsT[:, k, :],
                                           start=(k == 0), stop=(k == KT - 1))
                        mm.then_inc(h_done, 1)
                    turn_x(tile + 1)
                    pe.wait_ge(y_ready, tile + 1)
                    for m in range(2):
                        pe.wait_ge(hu_ready, 2 * tile + m + 1)
                        mm = pe.matmul(bank[3][:, :], hu[:, m, :], w2[par][:, m, :], start=(m == 0), stop=(m == 1))
                    mm.then_inc(y2_done, 1)

            for par in range(WB):
                expert(0, par)
            with pe.Fori(1, EXP // WB) as four:
                for par in range(WB):
                    expert(four, par)


def tile_of(tiles, g):
    if isinstance(g, int):
        return tiles[g]
    return tiles[bass.ds(g, 1)].rearrange("o a b c -> (o a) b c" if len(tiles.shape) == 4 else "o a b -> (o a) b")


_LAYOUTS = ("s4d", "c_tiles", "w_dt", "w_bx", "w_c", "w_r", "w_o", "w_rt", "w_s1", "w_s2", "br", "experts")


def layouts(x, log_dt, B_ri, inv_A_real, A_imag, w_in, w_param, w_out, Wr, br, W1, W2, Ws1, Ws2):
    def rows(a):
        return a.reshape(NT, 2, J, DS).transpose(1, 3, 0, 2).reshape(P, P)

    def contract(w):
        o, i = w.shape
        return np.ascontiguousarray(w.T.reshape(i // P, P, o).transpose(1, 0, 2))

    s4d = np.stack([rows(inv_A_real), rows(A_imag), rows(np.broadcast_to(log_dt[:, None], (NH, DS))),
                    rows(B_ri[..., 0]), rows(B_ri[..., 1])], axis=1)
    c = x.reshape(NB, NT, 2, J, DS, 2).transpose(1, 2, 4, 5, 3, 0).reshape(NT, P, 2, J * NB)
    wp = w_param.reshape(HEADS, 1 + 2 * DS, D)
    wi = w_in.reshape(2, HEADS, DH, D)
    w_bx = np.concatenate([wp[:, 1:1 + DS], wi[0]], axis=1).reshape(HEADS * P, D)
    d = {
        "s4d": s4d, "c_tiles": c, "w_bx": contract(w_bx), "w_c": contract(wp[:, 1 + DS:].reshape(HEADS * DS, D)),
        "w_r": contract(wi[1].reshape(HEADS * DH, D)),
        "w_dt": contract(np.broadcast_to(wp[None, :, 0], (J, HEADS, D)).reshape(P, D)),
        "w_o": contract(w_out), "w_rt": contract(Wr), "w_s1": contract(Ws1), "w_s2": contract(Ws2),
        "br": np.broadcast_to(br[None, :], (P, EXP)),
        "experts": np.stack([np.concatenate([contract(W1[e]).reshape(P, -1), contract(W2[e]).reshape(P, -1)], axis=1)
                             for e in range(EXP)]),
    }
    return {k: np.ascontiguousarray(v) for k, v in d.items()}


def kernel(x, L0_tok_log_dt, L0_tok_B_ri, L0_tok_inv_A_real, L0_tok_A_imag, L0_attn_w_in, L0_attn_w_param,
           L0_attn_w_out, L0_ffn_Wr, L0_ffn_br, L0_ffn_W1, L0_ffn_W2, L0_ffn_Ws1, L0_ffn_Ws2):
    import concourse.bacc as bacc
    from concourse.bass_utils import run_bass_kernel_spmd

    arrays = layouts(*(np.asarray(a) for a in (
        x, L0_tok_log_dt, L0_tok_B_ri, L0_tok_inv_A_real, L0_tok_A_imag, L0_attn_w_in, L0_attn_w_param,
        L0_attn_w_out, L0_ffn_Wr, L0_ffn_br, L0_ffn_W1, L0_ffn_W2, L0_ffn_Ws1, L0_ffn_Ws2)))
    nc = bacc.Bacc("TRN2", target_bir_lowering=False, num_devices=1)
    t = {k: nc.dram_tensor(f"in_{k}", a.shape, F32, kind="ExternalInput").ap() for k, a in arrays.items()}
    t["out"] = nc.dram_tensor("out_0", (NB, NH, D), F32, kind="ExternalOutput").ap()
    build(nc, t)
    r = run_bass_kernel_spmd(nc, [{f"in_{k}": a for k, a in arrays.items()}], core_ids=[0])
    return r.results[0]["out_0"]
```
